# Optimizing a Trainium2 kernel written in Bass

```python
import numpy as np
import jax
import jax.numpy as jnp

def _softmax(x, axis=-1):
    return jax.nn.softmax(x, axis=axis)

def _gelu(x):
    return jax.nn.gelu(x, approximate=True)

def _silu(x):
    return jax.nn.silu(x)

def _sigmoid(x):
    return jax.nn.sigmoid(x)

def _layernorm(x, axis=-1, eps=1e-05):
    m = jnp.mean(x, axis=axis, keepdims=True)
    v = jnp.var(x, axis=axis, keepdims=True)
    return (x - m) / jnp.sqrt(v + eps)

def _scatter_add(tgt, idx, src, axis=0):
    return tgt.at[idx].add(src)

def _segment_sum(src, seg, n):
    return jax.ops.segment_sum(src, seg, n)
kernel_name = 'mk_prb_d1_jaxref_r4_d640e3'

def setup_inputs(seed: int=0):
    np.random.seed(seed)
    _w = jnp.asarray

    def _L0_attn_setup():
        import jax, jax.numpy as jnp
        import numpy as np
        CHUNK = 64
        EPS_K = 1e-12
        NORM_EPS = 1e-05
        SCALE = 64 ** (-0.5)

        def gla_chunk_scan(q, k, v, g):
            B, T, K = q.shape
            V = v.shape[-1]
            nC = T // CHUNK

            def to_chunks(x):
                return x.reshape(B, nC, CHUNK, x.shape[-1]).transpose(1, 0, 2, 3)
            qc, kc, vc, gc = map(to_chunks, (q, k, v, g))
            mask = jnp.tril(jnp.ones((CHUNK, CHUNK), dtype=bool))[None, :, :, None]

            def body(S, xs):
                qt, kt, vt, gt = xs
                b = jnp.cumsum(gt, axis=1)
                o_inter = jnp.einsum('bck,bkv->bcv', qt * jnp.exp(b), S)
                diff = b[:, :, None, :] - b[:, None, :, :]
                D = jnp.exp(jnp.where(mask, diff, -jnp.inf))
                A = jnp.einsum('bik,bjk,bijk->bij', qt, kt, D)
                o = o_inter + jnp.einsum('bij,bjv->biv', A, vt)
                btot = b[:, -1, :]
                k_dec = kt * jnp.exp(btot[:, None, :] - b)
                S = jnp.exp(btot)[:, :, None] * S + jnp.einsum('bck,bcv->bkv', k_dec, vt)
                return (S, o)
            S0 = jnp.zeros((B, K, V), dtype=q.dtype)
            _, oc = jax.lax.scan(body, S0, (qc, kc, vc, gc))
            return oc.transpose(1, 0, 2, 3).reshape(B, T, V)
        key = jax.random.key(seed)
        B, T, H = (4, 512, 256)
        Di, K, R, W = (512, 64, 16, 4)
        ks = jax.random.split(key, 14)
        s = 0.02
        return {'hidden_states': jax.random.normal(ks[0], (B, T, H), jnp.float32), 'up_w': jax.random.normal(ks[1], (Di, H), jnp.float32) * s, 'gate_w': jax.random.normal(ks[2], (Di, H), jnp.float32) * s, 'conv_w': jax.random.normal(ks[3], (Di, W), jnp.float32) * 0.2, 'conv_b': jax.random.normal(ks[4], (Di,), jnp.float32) * s, 'q_w': jax.random.normal(ks[5], (K, Di), jnp.float32) * s, 'k_w': jax.random.normal(ks[6], (K, Di), jnp.float32) * s, 'g_w': jax.random.normal(ks[7], (K, Di), jnp.float32) * s, 'g_b': jnp.zeros((K,), jnp.float32), 'tau_w': jax.random.normal(ks[8], (K, Di), jnp.float32) * s, 'tau_b': jnp.zeros((K,), jnp.float32), 'ig_w1': jax.random.normal(ks[9], (R, Di), jnp.float32) * s, 'ig_w2': jax.random.normal(ks[10], (Di, R), jnp.float32) * 0.05, 'ig_b2': jnp.zeros((Di,), jnp.float32), 'residual_weight': jnp.ones((Di,), jnp.float32), 'norm_weight': jnp.ones((Di,), jnp.float32), 'down_w': jax.random.normal(ks[11], (H, Di), jnp.float32) * s}
    _L0_attn_in = _L0_attn_setup()

    def _L0_ffn_setup():
        import jax, jax.numpy as jnp
        import numpy as np
        D_IN, D_HID = (256, 1024)

        def _ternary(key, shape):
            return jax.random.randint(key, shape, -1, 2).astype(jnp.float32)

        def _tlin(x, w, s):
            return jnp.einsum('bsi,oi->bso', x, w) * s
        key = jax.random.key(seed)
        ks = jax.random.split(key, 12)
        inv = lambda fan: 1.0 / np.sqrt(fan).astype(np.float32)
        return {'x': jax.random.normal(ks[0], (4, 512, D_IN), dtype=jnp.float32), 'w1_w': _ternary(ks[1], (D_HID, D_IN)), 'w1_s': jax.random.uniform(ks[2], (D_HID,), dtype=jnp.float32) * inv(D_IN), 'w2_w': _ternary(ks[3], (D_HID, D_IN)), 'w2_s': jax.random.uniform(ks[4], (D_HID,), dtype=jnp.float32) * inv(D_IN), 'h1_w': _ternary(ks[5], (D_HID, D_HID)), 'h1_s': jax.random.uniform(ks[6], (D_HID,), dtype=jnp.float32) * inv(D_HID), 'h2_w': _ternary(ks[7], (D_HID, D_HID)), 'h2_s': jax.random.uniform(ks[8], (D_HID,), dtype=jnp.float32) * inv(D_HID), 'w3_w': _ternary(ks[9], (D_IN, D_HID)), 'w3_s': jax.random.uniform(ks[10], (D_IN,), dtype=jnp.float32) * inv(D_HID)}
    _L0_ffn_in = _L0_ffn_setup()
    _d = {'L0_attn_hidden_states': _L0_attn_in['hidden_states'], 'L0_attn_up_w': _L0_attn_in['up_w'], 'L0_attn_gate_w': _L0_attn_in['gate_w'], 'L0_attn_conv_w': _L0_attn_in['conv_w'], 'L0_attn_conv_b': _L0_attn_in['conv_b'], 'L0_attn_q_w': _L0_attn_in['q_w'], 'L0_attn_k_w': _L0_attn_in['k_w'], 'L0_attn_g_w': _L0_attn_in['g_w'], 'L0_attn_g_b': _L0_attn_in['g_b'], 'L0_attn_tau_w': _L0_attn_in['tau_w'], 'L0_attn_tau_b': _L0_attn_in['tau_b'], 'L0_attn_ig_w1': _L0_attn_in['ig_w1'], 'L0_attn_ig_w2': _L0_attn_in['ig_w2'], 'L0_attn_ig_b2': _L0_attn_in['ig_b2'], 'L0_attn_residual_weight': _L0_attn_in['residual_weight'], 'L0_attn_norm_weight': _L0_attn_in['norm_weight'], 'L0_attn_down_w': _L0_attn_in['down_w'], 'L0_ffn_w1_w': _L0_ffn_in['w1_w'], 'L0_ffn_w1_s': _L0_ffn_in['w1_s'], 'L0_ffn_w2_w': _L0_ffn_in['w2_w'], 'L0_ffn_w2_s': _L0_ffn_in['w2_s'], 'L0_ffn_h1_w': _L0_ffn_in['h1_w'], 'L0_ffn_h1_s': _L0_ffn_in['h1_s'], 'L0_ffn_h2_w': _L0_ffn_in['h2_w'], 'L0_ffn_h2_s': _L0_ffn_in['h2_s'], 'L0_ffn_w3_w': _L0_ffn_in['w3_w'], 'L0_ffn_w3_s': _L0_ffn_in['w3_s']}
    _x0 = _d['L0_attn_hidden_states']
    _d['L0_attn_hidden_states'] = jax.random.normal(jax.random.fold_in(jax.random.key(seed), 1), (16, 512, 256), dtype=_x0.dtype)
    del _x0
    return _d

def reference(L0_attn_hidden_states, L0_attn_up_w, L0_attn_gate_w, L0_attn_conv_w, L0_attn_conv_b, L0_attn_q_w, L0_attn_k_w, L0_attn_g_w, L0_attn_g_b, L0_attn_tau_w, L0_attn_tau_b, L0_attn_ig_w1, L0_attn_ig_w2, L0_attn_ig_b2, L0_attn_residual_weight, L0_attn_norm_weight, L0_attn_down_w, L0_ffn_w1_w, L0_ffn_w1_s, L0_ffn_w2_w, L0_ffn_w2_s, L0_ffn_h1_w, L0_ffn_h1_s, L0_ffn_h2_w, L0_ffn_h2_s, L0_ffn_w3_w, L0_ffn_w3_s):

    def _L0_attn_ref(hidden_states, up_w, gate_w, conv_w, conv_b, q_w, k_w, g_w, g_b, tau_w, tau_b, ig_w1, ig_w2, ig_b2, residual_weight, norm_weight, down_w):
        import jax, jax.numpy as jnp
        import numpy as np
        CHUNK = 64
        EPS_K = 1e-12
        NORM_EPS = 1e-05
        SCALE = 64 ** (-0.5)

        def gla_chunk_scan(q, k, v, g):
            B, T, K = q.shape
            V = v.shape[-1]
            nC = T // CHUNK

            def to_chunks(x):
                return x.reshape(B, nC, CHUNK, x.shape[-1]).transpose(1, 0, 2, 3)
            qc, kc, vc, gc = map(to_chunks, (q, k, v, g))
            mask = jnp.tril(jnp.ones((CHUNK, CHUNK), dtype=bool))[None, :, :, None]

            def body(S, xs):
                qt, kt, vt, gt = xs
                b = jnp.cumsum(gt, axis=1)
                o_inter = jnp.einsum('bck,bkv->bcv', qt * jnp.exp(b), S)
                diff = b[:, :, None, :] - b[:, None, :, :]
                D = jnp.exp(jnp.where(mask, diff, -jnp.inf))
                A = jnp.einsum('bik,bjk,bijk->bij', qt, kt, D)
                o = o_inter + jnp.einsum('bij,bjv->biv', A, vt)
                btot = b[:, -1, :]
                k_dec = kt * jnp.exp(btot[:, None, :] - b)
                S = jnp.exp(btot)[:, :, None] * S + jnp.einsum('bck,bcv->bkv', k_dec, vt)
                return (S, o)
            S0 = jnp.zeros((B, K, V), dtype=q.dtype)
            _, oc = jax.lax.scan(body, S0, (qc, kc, vc, gc))
            return oc.transpose(1, 0, 2, 3).reshape(B, T, V)
        B, T, H = hidden_states.shape
        x = hidden_states @ up_w.T
        final_gate = hidden_states @ gate_w.T
        W = conv_w.shape[1]
        xp = jnp.pad(x, ((0, 0), (W - 1, 0), (0, 0)))
        shift = sum((xp[:, j:j + T, :] * conv_w[:, j] for j in range(W))) + conv_b
        shift = jax.nn.silu(shift)
        q = shift @ q_w.T
        k = shift @ k_w.T
        v = jax.nn.sigmoid(x @ ig_w1.T @ ig_w2.T + ig_b2) * x
        g_gate = jax.nn.softplus(shift @ g_w.T + g_b)
        tau = jax.nn.sigmoid(shift @ tau_w.T + tau_b)
        it_gate = g_gate ** tau
        rt_log = -g_gate * tau
        kn = k / jnp.maximum(jnp.linalg.norm(k, axis=-1, keepdims=True), EPS_K) * it_gate
        o = gla_chunk_scan(q * SCALE, kn, v, rt_log)
        o = o + shift * residual_weight
        xg = o * jax.nn.silu(final_gate)
        rms = jax.lax.rsqrt(jnp.mean(xg * xg, axis=-1, keepdims=True) + NORM_EPS)
        o = xg * rms * norm_weight
        return o @ down_w.T

    def _L0_ffn_ref(x, w1_w, w1_s, w2_w, w2_s, h1_w, h1_s, h2_w, h2_s, w3_w, w3_s):
        import jax, jax.numpy as jnp
        import numpy as np
        D_IN, D_HID = (256, 1024)

        def _ternary(key, shape):
            return jax.random.randint(key, shape, -1, 2).astype(jnp.float32)

        def _tlin(x, w, s):
            return jnp.einsum('bsi,oi->bso', x, w) * s
        h = jax.nn.silu(_tlin(x, w1_w, w1_s)) * _tlin(x, w2_w, w2_s)
        h = jax.nn.gelu(_tlin(h, h1_w, h1_s), approximate=False)
        h = jax.nn.gelu(_tlin(h, h2_w, h2_s), approximate=False)
        return _tlin(h, w3_w, w3_s)
    x = L0_attn_hidden_states
    xn = _layernorm(x, axis=-1)
    x = x + _L0_attn_ref(xn, L0_attn_up_w, L0_attn_gate_w, L0_attn_conv_w, L0_attn_conv_b, L0_attn_q_w, L0_attn_k_w, L0_attn_g_w, L0_attn_g_b, L0_attn_tau_w, L0_attn_tau_b, L0_attn_ig_w1, L0_attn_ig_w2, L0_attn_ig_b2, L0_attn_residual_weight, L0_attn_norm_weight, L0_attn_down_w) + _L0_ffn_ref(xn, L0_ffn_w1_w, L0_ffn_w1_s, L0_ffn_w2_w, L0_ffn_w2_s, L0_ffn_h1_w, L0_ffn_h1_s, L0_ffn_h2_w, L0_ffn_h2_s, L0_ffn_w3_w, L0_ffn_w3_s)
    return x

_drawn_inputs = setup_inputs


def setup_inputs(seed=0):
    import zlib

    import numpy as np

    out = dict(_drawn_inputs(seed))
    spreads = {'L0_attn_g_b': (0.0, 0.1),
     'L0_attn_tau_b': (0.0, 0.1),
     'L0_attn_ig_b2': (0.0, 0.1),
     'L0_attn_residual_weight': (1.0, 0.2),
     'L0_attn_norm_weight': (1.0, 0.2)}
    factors = {}
    for name, (base, spread) in spreads.items():
        noise = np.random.default_rng([zlib.crc32(name.encode()), seed]).standard_normal(out[name].shape)
        drawn = base * np.exp(spread * noise) if base else spread * noise
        out[name] = jnp.asarray(drawn.astype(out[name].dtype))
    for name, factor in factors.items():
        out[name] = (out[name] * factor).astype(out[name].dtype)
    return out
```

```python
from contextlib import ExitStack

import concourse.bass as bass
import numpy as np
from concourse import mybir

F32 = mybir.dt.float32
F32R = mybir.dt.float32r
ALU = mybir.AluOpType
ACT = mybir.ActivationFunctionType

P = 128
B, T, H = 16, 512, 256
DI, K, R, W = 512, 64, 16, 4
F = 1024
CH = 128
NC = 2
N = CH * NC
HALVES = T // N
HB, DB, FB = H // P, DI // P, F // P
LEVELS = 7
UP = CH // 2
EPS = 1e-5
KEPS2 = 1e-24
STAGE = 1024
SLOTS = 4
LOG_DEG = 10

CHUNKS = (["comb", "up"] + [f"w1{k}" for k in range(2)] + [f"w2{k}" for k in range(2)] + ["gate", "proj"]
          + [f"h1{k}" for k in range(8)] + [f"h2{k}" for k in range(8)] + ["down", "w30", "w31"])
SPLIT = {"up": 0, "gate": 1, "proj": 2, "down": 3}
WHOLE = {n: i for i, n in enumerate(c for c in CHUNKS if c not in SPLIT and c != "comb")}


def log1p_ratio():
    e = (np.cos(np.pi * (np.arange(400) + 0.5) / 400) + 1) / 2
    c = np.polynomial.Chebyshev.fit(e, np.log1p(e) / e, LOG_DEG, domain=[0, 1])
    return [float(x) for x in c.convert(kind=np.polynomial.Polynomial).coef]


class Signal:

    def __init__(self, sem, per_half, primed=0):
        self.sem, self.n, self.primed = sem, per_half, primed

    def at(self, half, k=None):
        seq, place = half
        k = self.n if k is None else k
        return seq * (HALVES * self.n) + (place * self.n + k + self.primed)


def layer_program(nc, x, stage_w, ig1t, ig2t, convw, convb, projb, resw, normw, s1, s2, sh1, sh2, s3, ident,
                  masks, restart, out):
    ctx = ExitStack()
    with ctx:
        def sb(name, shape, dt=F32):
            return ctx.enter_context(nc.sbuf_tensor(name, shape, dt))

        def sig(name, per_half, primed=0):
            return Signal(ctx.enter_context(nc.semaphore(name)), per_half, primed)

        def sem(name):
            return ctx.enter_context(nc.semaphore(name))

        wwhole = sb("wwhole", [P, len(WHOLE), STAGE], F32R)
        whi = sb("whi", [P, len(SPLIT), STAGE], F32R)
        wlo = sb("wlo", [P, len(SPLIT), STAGE], F32R)
        combh = sb("combh", [P, HB, R], F32R)
        combl = sb("combl", [P, HB, R], F32R)
        combw = sb("combw", [P, HB, R])
        ig1w = sb("ig1w", [P, DB, R])
        ig2w = sb("ig2w", [R + 1, DI])
        convw_s = sb("convw_s", [P, DB, W])
        convb_s = sb("convb_s", [P, DB])
        projb_s = sb("projb_s", [P, 1])
        projb_half = sb("projb_half", [P, 1])
        resw_s = sb("resw_s", [P, DB])
        normw_s = sb("normw_s", [P, DB])
        s1_s, s2_s = sb("s1_s", [P, FB]), sb("s2_s", [P, FB])
        sh1_s, sh2_s = sb("sh1_s", [P, FB]), sb("sh2_s", [P, FB])
        s3_s = sb("s3_s", [P, H])
        ident_s = sb("ident_s", [P, P])
        masks_s = sb("masks_s", [P, LEVELS, UP])
        restart_s = sb("restart_s", [K, N])
        ones = sb("ones", [P, 1])
        minus_half = sb("minus_half", [P, NC])

        xin = sb("xin", [P, HALVES, NC, H])
        xnth, xntl = sb("xnth", [P, HB, N], F32R), sb("xntl", [P, HB, N], F32R)
        hid0h, hid0l = sb("hid0h", [P, FB, N], F32R), sb("hid0l", [P, FB, N], F32R)
        hid1h, hid1l = sb("hid1h", [P, FB, N], F32R), sb("hid1l", [P, FB, N], F32R)
        mixed = sb("mixed", [P, NC * LEVELS * UP])
        silu1 = mixed[:, 0:2 * N].rearrange("p (a t) -> p a t", a=2)
        mprod = mixed[:].rearrange("p (c l u) -> p c l u", c=NC, l=LEVELS)
        ffn = mixed[:, 0:NC * H].rearrange("p (c h) -> p c h", c=NC)
        raw = sb("raw", [P, 2, 2, N])
        xbuf = sb("xbuf", [P, DB, W - 1 + N])
        shift = sb("shift", [P, DB, N])
        parth, partl = sb("parth", [P, DB, N], F32R), sb("partl", [P, DB, N], F32R)
        sgate = sb("sgate", [P, DB, N])
        zb = sb("zb", [R + 1, N])
        v = sb("v", [P, NC, DI])
        small = sb("small", [K, 8, N])
        work = sb("work", [P, LEVELS * N + LEVELS * N // 2])
        tanhv = work[:, 0:NC * DI].rearrange("p (c d) -> p c d", c=NC)
        lev = work[0:K, 0:LEVELS * N].rearrange("p (l t) -> p l t", l=LEVELS)
        levq = work[0:K, LEVELS * N:LEVELS * N + LEVELS * N // 2].rearrange("p (l t) -> p l t", l=LEVELS)
        sq = work[:, 0:DB * N].rearrange("p (d t) -> p d t", d=DB)
        xn = work[:, DB * N:DB * N + NC * H].rearrange("p (c h) -> p c h", c=NC)
        att = sb("att", [P, NC, CH])
        state = sb("state", [K, DI])
        kdt = sb("kdt", [P, NC, K])
        stats = sb("stats", [P, NC, 6])
        mv = sb("mv", [P, NC, 2])
        varp, rstd = sb("varp", [P, NC]), sb("rstd", [P, NC])
        ssk, rkn = sb("ssk", [P, NC]), sb("rkn", [P, NC])
        msq, rms = sb("msq", [P, NC]), sb("rms", [P, NC])
        nbt, decay = sb("nbt", [K, NC]), sb("decay", [K, NC])

        fb = [ctx.enter_context(nc.psum_tensor(f"fb{i}", [P, 512], F32)) for i in range(4)]
        ab = [ctx.enter_context(nc.psum_tensor(f"ab{i}", [P, 512], F32)) for i in range(4)]

        const_in = sem("const_in")
        stage_in = [sem(f"stage_in{i}") for i in range(SLOTS)]
        prep_act, prep_dve, prep_pe, prep_pool = sem("prep_act"), sem("prep_dve"), sem("prep_pe"), sem("prep_pool")
        x_in = [sem(f"x_in{i}") for i in range(HALVES)]
        x_out = [sem(f"x_out{i}") for i in range(HALVES)]
        up_mm, z_mm, l1_mm, gate_mm = sig("up_mm", 2), sig("z_mm", 1), sig("l1_mm", FB), sig("gate_mm", 2)
        xt_mm, ig_mm, pr_mm, dg_mm = sig("xt_mm", NC), sig("ig_mm", NC), sig("pr_mm", 1), sig("dg_mm", 1)
        lv_mm, kt_mm, ot_mm, su_mm = sig("lv_mm", NC), sig("kt_mm", 1), sig("ot_mm", NC), sig("su_mm", NC)
        h1_mm, h2_mm, dn_mm = sig("h1_mm", 4), sig("h2_mm", 4), sig("dn_mm", 1)
        rs_mm, ln_mm, w3_mm = sig("rs_mm", 1), sig("ln_mm", 1, 1), sig("w3_mm", 1)
        x_ev, z_ev, tap0, silu_d = sig("x_ev", 2), sig("z_ev", 1), sig("tap0", DB), sig("silu_d", FB)
        hid0_hi, gate_ev, shift_d, shift_hi = sig("hid0_hi", 4), sig("gate_ev", 2), sig("shift_d", 1), sig("shift_hi", 1)
        tanh_d, qk_ev, exp_d, ln_d, it_d = sig("tanh_d", NC), sig("qk_ev", 4), sig("exp_d", 2), sig("ln_d", 1), sig("it_d", 1)
        lev_d, dec_d, kd_ev = sig("lev_d", 1), sig("dec_d", 4), sig("kd_ev", NC)
        gelu1_d, hid1_hi, gelu2_d, hid2_hi = sig("gelu1_d", FB), sig("hid1_hi", 4), sig("gelu2_d", FB), sig("hid2_hi", 4)
        sq_d, xg_hi, ln_hi = sig("sq_d", 1), sig("xg_hi", 1), sig("ln_hi", 1, 1)
        conv_d, l1_d, hid0_lo, shift_lo = sig("conv_d", DB * (W - 1)), sig("l1_d", FB), sig("hid0_lo", 4), sig("shift_lo", 1)
        halo_d = sig("halo_d", 1, 1)
        v_d, gs = sig("v_d", NC), sig("gs", LOG_DEG + 14)
        levarg_d, levq_d, levk_d, kd_d, qd_d = sig("levarg_d", 1), sig("levq_d", 1), sig("levk_d", 1), sig("kd_d", 1), sig("qd_d", 1)
        ss_d, att_d, mask_d = sig("ss_d", 1), sig("att_d", LEVELS + 2), sig("mask_d", NC)
        st_d, o_d, xg_d, xg_lo = sig("st_d", NC), sig("o_d", NC, NC), sig("xg_d", 1), sig("xg_lo", 1)
        hid1_lo, hid2_lo = sig("hid1_lo", 4), sig("hid2_lo", 4)
        msq_d, fin_d, stat_d, var_d, xn_d, ln_lo = (sig("msq_d", 1, 1), sig("fin_d", 4, 4), sig("stat_d", 3, 3),
                                                    sig("var_d", 1, 1), sig("xn_d", 1, 1), sig("ln_lo", 1, 1))
        rkn_d, rms_d, rstd_d = sig("rkn_d", 1), sig("rms_d", 1), sig("rstd_d", 1, 1)

        q_s, k_s, bsum, t1, t2, t3, t4, t5 = (small[:, i, :] for i in range(8))
        CONSTS = [(ig1w, ig1t), (ig2w, ig2t), (convw_s, convw), (convb_s, convb), (projb_s, projb), (resw_s, resw),
                  (normw_s, normw), (s1_s, s1), (s2_s, s2), (sh1_s, sh1), (sh2_s, sh2), (s3_s, s3), (ident_s, ident),
                  (masks_s, masks), (restart_s, restart)]

        def ready(names):
            return max(CHUNKS.index(n) for n in names) + 1

        def stage_slot(n):
            return (sgate[:].rearrange("p d t -> p (d t)"), shift[:].rearrange("p d t -> p (d t)"),
                    v[:].rearrange("p c d -> p (c d)"), raw[:].rearrange("p a b t -> p (a b t)"))[n % SLOTS]

        def levels(ap, m):
            return ap.rearrange("p (b u r) -> p b u r", u=2, r=m)

        block = ctx.enter_context(nc.Block())

        @block.sync
        def _(sp):
            sp.sem_inc(x_out[1], 16)
            sp.dma_start(xin[:, 0, :, :], x[0]).then_inc(x_in[0], 16)
            for dst, src in CONSTS:
                sp.dma_start(dst[:], src).then_inc(const_in, 16)
            for n in range(len(CHUNKS)):
                if n >= SLOTS:
                    sp.wait_ge(prep_act, n - SLOTS + 1)
                    sp.wait_ge(prep_dve, n - SLOTS + 1)
                sp.dma_start(stage_slot(n), stage_w[n]).then_inc(stage_in[n % SLOTS], 16)

            def half(seq, p, last):
                me = (seq, p)
                if not (last and p == HALVES - 1):
                    if p == 0:
                        sp.wait_ge(x_out[1], seq * 16 + 16)
                        sp.dma_start(xin[:, 1, :, :], x[seq * HALVES + 1]).then_inc(x_in[1], 16)
                    else:
                        sp.wait_ge(x_out[0], seq * 16 + 16)
                        sp.dma_start(xin[:, 0, :, :], x[seq * HALVES + HALVES]).then_inc(x_in[0], 16)
                sp.wait_ge(fin_d.sem, fin_d.at(me))
                sp.dma_start(out[seq * HALVES + p], xin[:, p, :, :]).then_inc(x_out[p], 16)

            with sp.Fori(0, B - 1) as seq:
                for p in range(HALVES):
                    half(seq, p, False)
            for p in range(HALVES):
                half(B - 1, p, True)
            sp.wait_ge(x_out[0], B * 16)
            sp.wait_ge(x_out[1], B * 16 + 16)

        @block.gpsimd
        def _(pool):
            pool.memset(minus_half[:], -0.5).then_inc(prep_pool, 1)
            pool.memset(ones[:], 1.0).then_inc(prep_pool, 1)
            pool.memset(zb[:], 1.0).then_inc(prep_pool, 1)
            pool.memset(xbuf[:], 0.0).then_inc(prep_pool, 1)
            pool.wait_ge(prep_pool, 1)

            def normalise(me):
                pool.wait_ge(var_d.sem, var_d.at(me))
                pool.tensor_tensor(rstd[:], varp[:], minus_half[:], ALU.pow).then_inc(rstd_d.sem, 1)

            def half(seq, p, last):
                me = (seq, p)
                pool.wait_ge(ss_d.sem, ss_d.at(me))
                pool.tensor_tensor(rkn[:], ssk[:], minus_half[:], ALU.pow).then_inc(rkn_d.sem, 1)
                if not (last and p == HALVES - 1):
                    normalise(me)
                pool.wait_ge(msq_d.sem, msq_d.at(me))
                pool.tensor_tensor(rms[:], msq[:], minus_half[:], ALU.pow).then_inc(rms_d.sem, 1)

            normalise((0, -1))
            with pool.Fori(0, B - 1) as seq:
                for p in range(HALVES):
                    half(seq, p, False)
            for p in range(HALVES):
                half(B - 1, p, True)

        @block.tensor
        def _(pe):
            def wide(o, pairs, start=True, stop=True):
                for i, (a, b) in enumerate(pairs):
                    mm = pe.matmul(o, a, b, start=start and i == 0, stop=stop and i == len(pairs) - 1)
                return mm

            def three(whi_b, wlo_b, ah, al):
                return [(whi_b, ah), (whi_b, al), (wlo_b, ah)]

            def split_w(name, k, lo, hi, width):
                i = SPLIT[name]
                return whi[:, i, k * width + lo:k * width + hi], wlo[:, i, k * width + lo:k * width + hi]

            def fw(name, k, lo, hi):
                return wwhole[:, WHOLE[f"{name}{k}"], lo:hi]

            pe.wait_ge(const_in, 16 * len(CONSTS))
            pe.wait_ge(stage_in[0], 16)
            for h in range(HB):
                for d in range(DB):
                    mm = pe.matmul(ab[0][:, h * R:(h + 1) * R], stage_slot(0)[:, d * H + h * P:d * H + (h + 1) * P],
                                   ig1w[:, d, :], start=(d == 0), stop=(d == DB - 1))
            mm.then_inc(prep_pe, 1)

            def ln_transpose(me, first=False):
                pe.wait_ge(xn_d.sem, xn_d.at(me))
                if not first:
                    pe.wait_ge(st_d.sem, st_d.at(me, 2))
                for h in range(HB):
                    for c in range(NC):
                        mm = pe.transpose(ab[2][:, h * N + c * CH:h * N + (c + 1) * CH], xn[:, c, h * P:(h + 1) * P], ident_s[:])
                mm.then_inc(ln_mm.sem, 1)

            ln_transpose((0, -1), True)

            def half(seq, p, last):
                me, prev = (seq, p), (seq, p - 1)
                xh, xl = xnth, xntl
                pe.wait_ge(ln_hi.sem, ln_hi.at(prev))
                pe.wait_ge(ln_lo.sem, ln_lo.at(prev))
                pe.wait_ge(prep_act, ready(["up"]))
                pe.wait_ge(prep_dve, ready(["up"]))
                for b in range(2):
                    pe.wait_ge(o_d.sem, o_d.at(prev, b + 1))
                    for m in (2 * b, 2 * b + 1):
                        pairs = []
                        for k in range(HB):
                            pairs += three(*split_w("up", k, m * P, (m + 1) * P, DI), xh[:, k, :], xl[:, k, :])
                        mm = wide(ab[b][:, (m % 2) * N:(m % 2 + 1) * N], pairs)
                    mm.then_inc(up_mm.sem, 1)
                pairs = []
                for k in range(HB):
                    pairs += three(combh[:, k, :], combl[:, k, :], xh[:, k, :], xl[:, k, :])
                wide(ab[2][0:R, 0:N], pairs).then_inc(z_mm.sem, 1)

                def layer1(m):
                    if m == 0:
                        pe.wait_ge(fin_d.sem, fin_d.at(prev))
                    elif m == 1:
                        pe.wait_ge(msq_d.sem, msq_d.at(prev))
                    elif m >= 4:
                        pe.wait_ge(l1_d.sem, l1_d.at(me, m - 3))
                    for j, w in enumerate(("w1", "w2")):
                        pairs = []
                        for k in range(HB):
                            wb = fw(w, k, m * P, (m + 1) * P)
                            pairs += [(wb, xh[:, k, :]), (wb, xl[:, k, :])]
                        mm = wide(fb[m % 4][:, j * N:(j + 1) * N], pairs)
                    mm.then_inc(l1_mm.sem, 1)

                def gate(b):
                    if b == 0:
                        pe.wait_ge(z_ev.sem, z_ev.at(me))
                    else:
                        pe.wait_ge(fin_d.sem, fin_d.at(prev, 2))
                    for m in (2 * b, 2 * b + 1):
                        pairs = []
                        for k in range(HB):
                            pairs += three(*split_w("gate", k, m * P, (m + 1) * P, DI), xh[:, k, :], xl[:, k, :])
                        mm = wide(ab[2 + b][:, (m % 2) * N:(m % 2 + 1) * N], pairs)
                    mm.then_inc(gate_mm.sem, 1)

                pe.wait_ge(prep_act, ready(["w11", "w21"]))
                pe.wait_ge(prep_dve, ready(["w11", "w21"]))
                for m in range(4):
                    layer1(m)
                pe.wait_ge(prep_act, ready(["proj"]))
                pe.wait_ge(prep_dve, ready(["proj"]))
                gate(0)
                gate(1)
                for m in range(4, FB):
                    layer1(m)
                for c in range(NC):
                    pe.wait_ge(x_ev.sem, x_ev.at(me))
                    for d in range(DB):
                        mm = pe.transpose(ab[c][:, d * P:(d + 1) * P], xbuf[:, d, W - 1 + c * CH:W - 1 + (c + 1) * CH], ident_s[:])
                    mm.then_inc(xt_mm.sem, 1)
                for c in range(NC):
                    pe.wait_ge(gate_ev.sem, gate_ev.at(me, c + 1))
                    pe.matmul(ab[2 + c][:], zb[:, c * CH:(c + 1) * CH], ig2w[:], start=True, stop=True).then_inc(ig_mm.sem, 1)
                pe.wait_ge(shift_hi.sem, shift_hi.at(me))
                pe.wait_ge(shift_lo.sem, shift_lo.at(me))
                pe.wait_ge(tanh_d.sem, tanh_d.at(me, 1))
                for j in range(2):
                    pairs = []
                    for k in range(DB):
                        lo = j * DI + k * P
                        pairs += three(whi[:, SPLIT["proj"], lo:lo + P], wlo[:, SPLIT["proj"], lo:lo + P], parth[:, k, :], partl[:, k, :])
                    mm = wide(ab[2][:, j * N:(j + 1) * N], pairs)
                mm.then_inc(pr_mm.sem, 1)
                pe.wait_ge(hid0_hi.sem, hid0_hi.at(me))
                pe.wait_ge(hid0_lo.sem, hid0_lo.at(me))
                pe.wait_ge(prep_act, ready(["h17"]))
                pe.wait_ge(prep_dve, ready(["h17"]))

                def hidden(name, b, ih, il, done):
                    for m in (2 * b, 2 * b + 1):
                        pairs = []
                        for k in range(FB):
                            wb = fw(name, k, m * P, (m + 1) * P)
                            pairs += [(wb, ih[:, k, :]), (wb, il[:, k, :])]
                        mm = wide(fb[b][:, (m % 2) * N:(m % 2 + 1) * N], pairs)
                    mm.then_inc(done.sem, 1)

                for b in range(4):
                    pe.wait_ge(l1_d.sem, l1_d.at(me, b + 5))
                    hidden("h1", b, hid0h, hid0l, h1_mm)
                pe.wait_ge(gs.sem, gs.at(me))
                pe.wait_ge(qk_ev.sem, qk_ev.at(me))
                pe.wait_ge(tanh_d.sem, tanh_d.at(me, 2))
                for c in range(NC):
                    t = slice(c * CH, (c + 1) * CH)
                    pe.matmul(ab[3][:, c * CH:(c + 1) * CH], k_s[:, t], q_s[:, t], start=True, stop=True)
                for c in range(NC):
                    t = slice(c * CH, (c + 1) * CH)
                    mm = pe.matmul(ab[3][:, N + c:N + c + 1], t4[:, t], ones[0:K, :], start=True, stop=True)
                mm.then_inc(dg_mm.sem, 1)
                pe.wait_ge(kd_d.sem, kd_d.at(me))
                for c in range(NC):
                    pe.wait_ge(v_d.sem, v_d.at(me, c + 1))
                    pe.wait_ge(levq_d.sem, levq_d.at(me))
                    pe.wait_ge(levk_d.sem, levk_d.at(me))
                    for i in range(LEVELS):
                        mm = pe.matmul(ab[c][:, i * UP:(i + 1) * UP], lev[:, i, c * CH:(c + 1) * CH],
                                       levq[:, i, c * UP:(c + 1) * UP], start=True, stop=True)
                    mm.then_inc(lv_mm.sem, 1)
                for c in range(NC):
                    mm = pe.transpose(ab[2][:, c * K:(c + 1) * K], t5[:, c * CH:(c + 1) * CH], ident_s[0:K, 0:K])
                mm.then_inc(kt_mm.sem, 1)

                def outputs(c):
                    pe.wait_ge(mask_d.sem, mask_d.at(me, c + 1))
                    pe.wait_ge(att_d.sem, att_d.at(me))
                    carried = not (p == 0 and c == 0)
                    if carried:
                        pe.wait_ge(st_d.sem, st_d.at(me, 1) if c else st_d.at(prev, 2))
                        pe.wait_ge(qd_d.sem, qd_d.at(me))
                    for d in range(DB):
                        mm = pe.matmul(ab[c][:, d * CH:(d + 1) * CH], v[:, c, d * P:(d + 1) * P], att[:, c, :],
                                       start=True, stop=not carried)
                        if carried:
                            mm = pe.matmul(ab[c][:, d * CH:(d + 1) * CH], state[:, d * P:(d + 1) * P],
                                           t1[:, c * CH:(c + 1) * CH], start=False, stop=True)
                    mm.then_inc(ot_mm.sem, 1)
                    pe.wait_ge(kd_ev.sem, kd_ev.at(me))
                    pe.matmul(ab[3 - c][0:K, :], kdt[:, c, :], v[:, c, :], start=True, stop=True).then_inc(su_mm.sem, 1)

                pe.wait_ge(hid1_hi.sem, hid1_hi.at(me))
                pe.wait_ge(hid1_lo.sem, hid1_lo.at(me))
                pe.wait_ge(prep_act, ready(["h27"]))
                pe.wait_ge(prep_dve, ready(["h27"]))
                for b in range(4):
                    pe.wait_ge(gelu1_d.sem, gelu1_d.at(me, 2 * b + 2))
                    hidden("h2", b, hid1h, hid1l, h2_mm)
                    if b in (0, 1):
                        outputs(b)
                if not (last and p == HALVES - 1):
                    ln_transpose(me)
                pe.wait_ge(sq_d.sem, sq_d.at(me))
                pe.wait_ge(gelu2_d.sem, gelu2_d.at(me, 4))
                for c in range(NC):
                    for d in range(DB):
                        mm = pe.matmul(fb[1][:, c:c + 1], sq[:, d, c * CH:(c + 1) * CH], ones[:], start=(d == 0), stop=(d == DB - 1))
                mm.then_inc(rs_mm.sem, 1)
                pe.wait_ge(prep_act, ready(["w31"]))
                pe.wait_ge(prep_dve, ready(["w31"]))
                pe.wait_ge(xg_hi.sem, xg_hi.at(me))
                pe.wait_ge(xg_lo.sem, xg_lo.at(me))
                pe.wait_ge(st_d.sem, st_d.at(me, 1))
                for c in range(NC):
                    t = slice(c * CH, (c + 1) * CH)
                    pairs = []
                    for k in range(DB):
                        wh, wl = split_w("down", k, 0, H, H)
                        pairs += [(parth[:, k, t], wh), (partl[:, k, t], wh), (parth[:, k, t], wl)]
                    mm = wide(ab[3][:, c * H:(c + 1) * H], pairs)
                mm.then_inc(dn_mm.sem, 1)
                pe.wait_ge(hid2_hi.sem, hid2_hi.at(me))
                pe.wait_ge(hid2_lo.sem, hid2_lo.at(me))
                for c in range(NC):
                    t = slice(c * CH, (c + 1) * CH)
                    pairs = []
                    for k in range(FB):
                        wb = fw("w3", k // 4, (k % 4) * H, (k % 4 + 1) * H)
                        pairs += [(hid0h[:, k, t], wb), (hid0l[:, k, t], wb)]
                    mm = wide(fb[0][:, c * H:(c + 1) * H], pairs)
                mm.then_inc(w3_mm.sem, 1)

            pe.wait_ge(prep_pool, 4)
            with pe.Fori(0, B - 1) as seq:
                for p in range(HALVES):
                    half(seq, p, False)
            for p in range(HALVES):
                half(B - 1, p, True)

        @block.scalar
        def _(act):
            act.wait_ge(const_in, 16 * len(CONSTS))

            def ln_high(me):
                act.wait_ge(ln_mm.sem, ln_mm.at(me))
                if me[1] >= 0:
                    act.wait_ge(l1_mm.sem, l1_mm.at(me))
                act.activation(xnth[:], ab[2][:].rearrange("p (h t) -> p h t", h=HB), ACT.Copy).then_inc(ln_hi.sem, 1)

            for n, name in enumerate(CHUNKS):
                if name == "comb":
                    act.wait_ge(prep_pe, 1)
                    act.activation(combh[:], ab[0][:, 0:HB * R].rearrange("p (h r) -> p h r", h=HB), ACT.Copy).then_inc(prep_act, 1)
                    ln_high((0, -1))
                    continue
                act.wait_ge(stage_in[n % SLOTS], 16 * (n // SLOTS + 1))
                if name == "down":
                    for d in range(DB):
                        mul = act.activation(whi[:, SPLIT[name], d * H:(d + 1) * H], stage_slot(n)[:, d * H:(d + 1) * H], ACT.Copy,
                                             scale=normw_s[:, d:d + 1])
                    mul.then_inc(prep_act, 1)
                elif name in SPLIT:
                    act.activation(whi[:, SPLIT[name], :], stage_slot(n), ACT.Copy).then_inc(prep_act, 1)
                else:
                    act.activation(wwhole[:, WHOLE[name], 0:STAGE // 2], stage_slot(n)[:, 0:STAGE // 2], ACT.Copy).then_inc(prep_act, 1)

            def half(seq, p, last):
                me, prev = (seq, p), (seq, p - 1)

                for b in range(2):
                    act.wait_ge(up_mm.sem, up_mm.at(me, b + 1))
                    if b == 0:
                        act.wait_ge(halo_d.sem, halo_d.at(prev))
                    act.activation(xbuf[:, 2 * b:2 * b + 2, W - 1:], ab[b][:].rearrange("p (d t) -> p d t", d=2), ACT.Copy).then_inc(x_ev.sem, 1)
                act.wait_ge(z_mm.sem, z_mm.at(me))
                act.activation(zb[0:R, :], ab[2][0:R, 0:N], ACT.Copy).then_inc(z_ev.sem, 1)
                act.wait_ge(x_ev.sem, x_ev.at(me))
                for d in range(DB):
                    act.activation(shift[:, d, :], xbuf[:, d, 0:N], ACT.Identity, bias=convb_s[:, d:d + 1],
                                   scale=convw_s[:, d, 0:1]).then_inc(tap0.sem, 1)

                def high(src, dst, b, done):
                    act.activation(dst[:, 2 * b:2 * b + 2, :], src, ACT.Copy).then_inc(done.sem, 1)

                def silu(m):
                    act.wait_ge(l1_mm.sem, l1_mm.at(me, m + 1))
                    if m >= 2:
                        act.wait_ge(l1_d.sem, l1_d.at(me, m - 1))
                    act.activation(silu1[:, m % 2, :], fb[m % 4][:, 0:N], ACT.Silu, scale=s1_s[:, m:m + 1]).then_inc(silu_d.sem, 1)

                def hid0(b):
                    act.wait_ge(l1_d.sem, l1_d.at(me, 2 * b + 2))
                    high(raw[:, b % 2, :, :], hid0h, b, hid0_hi)

                for m in range(4):
                    silu(m)
                    if m == 3:
                        hid0(0)
                for b in range(2):
                    act.wait_ge(gate_mm.sem, gate_mm.at(me, b + 1))
                    act.activation(sgate[:, 2 * b:2 * b + 2, :], ab[2 + b][:].rearrange("p (d t) -> p d t", d=2), ACT.Silu).then_inc(gate_ev.sem, 1)
                for m in range(4, FB):
                    silu(m)
                    if m % 2:
                        hid0(m // 2 - 1)
                act.wait_ge(conv_d.sem, conv_d.at(me))
                act.activation(shift[:], shift[:], ACT.Silu).then_inc(shift_d.sem, 1)
                act.wait_ge(shift_d.sem, shift_d.at(me))
                act.activation(parth[:], shift[:], ACT.Copy).then_inc(shift_hi.sem, 1)
                hid0(3)
                for c in range(NC):
                    act.wait_ge(ig_mm.sem, ig_mm.at(me, c + 1))
                    act.activation(tanhv[:, c, :], ab[2 + c][:], ACT.Tanh, scale=0.5).then_inc(tanh_d.sem, 1)
                act.wait_ge(pr_mm.sem, pr_mm.at(me))
                act.activation(t3, ab[2][K:P, N:2 * N], ACT.Tanh, bias=projb_half[K:P, :], scale=0.5).then_inc(qk_ev.sem, 1)
                act.activation(k_s, ab[2][K:P, 0:N], ACT.Copy).then_inc(qk_ev.sem, 1)
                act.wait_ge(gs.sem, gs.at(me, 2))
                act.activation(q_s, ab[2][0:K, 0:N], ACT.Copy, scale=0.5 * K ** -0.5).then_inc(qk_ev.sem, 1)
                act.preload_act_table_set("natural_log_exp_and_others")
                act.wait_ge(gs.sem, gs.at(me, 3))
                act.activation(t4, t4, ACT.Exp).then_inc(exp_d.sem, 1)
                act.activation(t5, t1, ACT.Exp, scale=-1.0).then_inc(exp_d.sem, 1)
                act.wait_ge(gs.sem, gs.at(me, 3 + LOG_DEG + 4))
                act.activation(t5, t5, ACT.Ln).then_inc(ln_d.sem, 1)
                act.activation(t4, ab[2][K:P, 0:N], ACT.Square).then_inc(qk_ev.sem, 1)
                act.wait_ge(gs.sem, gs.at(me, 3 + LOG_DEG + 8))
                act.activation(t2, t2, ACT.Exp).then_inc(it_d.sem, 1)
                act.wait_ge(gs.sem, gs.at(me, LOG_DEG + 13))
                act.activation(t1, bsum, ACT.Exp, scale=-1.0).then_inc(dec_d.sem, 1)
                for c in range(NC):
                    t = slice(c * CH, (c + 1) * CH)
                    act.activation(t5[:, t], bsum[:, t], ACT.Exp, bias=nbt[:, c:c + 1]).then_inc(dec_d.sem, 1)
                act.activation(decay[:], nbt[:], ACT.Exp).then_inc(dec_d.sem, 1)
                act.wait_ge(levarg_d.sem, levarg_d.at(me))
                act.activation(lev[:], lev[:], ACT.Exp, scale=-1.0).then_inc(lev_d.sem, 1)
                def gelu(mm, scales, dst, b, done, done_hi, free):
                    act.wait_ge(mm.sem, mm.at(me, b + 1))
                    if free is not None:
                        act.wait_ge(*free)
                    for j in range(2):
                        act.activation(raw[:, b % 2, j, :], fb[b][:, j * N:(j + 1) * N], ACT.Gelu,
                                       scale=scales[:, 2 * b + j:2 * b + j + 1]).then_inc(done.sem, 1)
                    act.wait_ge(done.sem, done.at(me, 2 * b + 2))
                    high(raw[:, b % 2, :, :], dst, b, done_hi)

                for b in range(4):
                    lo = (hid0_lo, b + 3) if b < 2 else (hid1_lo, b - 1)
                    gelu(h1_mm, sh1_s, hid1h, b, gelu1_d, hid1_hi, (lo[0].sem, lo[0].at(me, lo[1])))
                act.wait_ge(kt_mm.sem, kt_mm.at(me))
                act.wait_ge(rkn_d.sem, rkn_d.at(me))
                for c in range(NC):
                    act.activation(kdt[:, c, :], ab[2][:, c * K:(c + 1) * K], ACT.Copy, scale=rkn[:, c:c + 1]).then_inc(kd_ev.sem, 1)
                for b in range(4):
                    lo = (hid1_lo, b + 3) if b < 2 else (hid2_lo, b - 1)
                    gelu(h2_mm, sh2_s, hid0h, b, gelu2_d, hid2_hi, (lo[0].sem, lo[0].at(me, lo[1])))
                    if b == 2:
                        act.wait_ge(xg_d.sem, xg_d.at(me))
                        act.activation(sq[:], sgate[:], ACT.Square).then_inc(sq_d.sem, 1)
                        act.activation(parth[:], sgate[:], ACT.Copy).then_inc(xg_hi.sem, 1)
                if not (last and p == HALVES - 1):
                    ln_high(me)

            act.wait_ge(prep_dve, len(CHUNKS))
            with act.Fori(0, B - 1) as seq:
                for p in range(HALVES):
                    half(seq, p, False)
            for p in range(HALVES):
                half(B - 1, p, True)

        @block.vector
        def _(dve):
            poly = log1p_ratio()
            for s in (o_d, fin_d, msq_d, halo_d):
                dve.sem_inc(s.sem, s.primed)

            def low(dst, src, hi):
                return dve.tensor_tensor(dst, src, hi.bitcast(F32), ALU.subtract)

            def statistics(me):
                seq, p = me
                if p == -1:
                    nxt = 0
                    dve.wait_ge(x_in[0], 16)
                else:
                    nxt = 1 - p
                    dve.wait_ge(x_in[nxt], seq * 16 + (16 if p == 0 else 32))
                for c in range(NC):
                    dve.bn_stats(stats[:, c, :], xin[:, nxt, c, :]).then_inc(stat_d.sem, 1)

            def variances(me):
                for c in range(NC):
                    ag = dve.bn_aggr(mv[:, c, :], stats[:, c, :])
                ag.then_inc(stat_d.sem, 1)
                dve.wait_ge(stat_d.sem, stat_d.at(me, 3))
                dve.tensor_scalar(varp[:], mv[:, :, 1], EPS, None, ALU.add).then_inc(var_d.sem, 1)

            def normalise(me):
                seq, p = me
                nxt = 0 if p == -1 else 1 - p
                dve.wait_ge(rstd_d.sem, rstd_d.at(me))
                for c in range(NC):
                    ts = dve.tensor_scalar(xn[:, c, :], xin[:, nxt, c, :], mv[:, c, 0:1], rstd[:, c:c + 1], ALU.subtract, ALU.mult)
                ts.then_inc(xn_d.sem, 1)

            def ln_low(me):
                dve.wait_ge(ln_hi.sem, ln_hi.at(me))
                low(xntl[:], ab[2][:].rearrange("p (h t) -> p h t", h=HB), xnth[:]).then_inc(ln_lo.sem, 1)

            dve.wait_ge(const_in, 16 * len(CONSTS))
            for n, name in enumerate(CHUNKS):
                if name == "comb":
                    dve.wait_ge(prep_pe, 1)
                    dve.wait_ge(prep_act, 1)
                    dve.tensor_scalar(projb_half[:], projb_s[:], 0.5, None, ALU.mult)
                    low(combl[:], ab[0][:, 0:HB * R].rearrange("p (h r) -> p h r", h=HB), combh[:]).then_inc(prep_dve, 1)
                    statistics((0, -1))
                    dve.wait_ge(stat_d.sem, stat_d.at((0, -1), 2))
                    variances((0, -1))
                    normalise((0, -1))
                    ln_low((0, -1))
                    continue
                dve.wait_ge(stage_in[n % SLOTS], 16 * (n // SLOTS + 1))
                if name in SPLIT:
                    dve.wait_ge(prep_act, n + 1)
                    if name == "down":
                        for d in range(DB):
                            t = slice(d * H, (d + 1) * H)
                            st = dve.scalar_tensor_tensor(wlo[:, SPLIT[name], t], stage_slot(n)[:, t], normw_s[:, d:d + 1],
                                                          whi[:, SPLIT[name], t].bitcast(F32), ALU.mult, ALU.subtract)
                        st.then_inc(prep_dve, 1)
                    else:
                        low(wlo[:, SPLIT[name], :], stage_slot(n), whi[:, SPLIT[name], :]).then_inc(prep_dve, 1)
                else:
                    dve.tensor_copy(wwhole[:, WHOLE[name], STAGE // 2:], stage_slot(n)[:, STAGE // 2:]).then_inc(prep_dve, 1)

            def half(seq, p, last):
                me, prev = (seq, p), (seq, p - 1)

                def layer1(m):
                    if m >= 4:
                        dve.wait_ge(hid0_lo.sem, hid0_lo.at(me, m // 2 - 1))
                    dve.wait_ge(silu_d.sem, silu_d.at(me, m + 1))
                    dve.scalar_tensor_tensor(raw[:, (m // 2) % 2, m % 2, :], fb[m % 4][:, N:2 * N], s2_s[:, m:m + 1],
                                             silu1[:, m % 2, :], ALU.mult, ALU.mult).then_inc(l1_d.sem, 1)

                def hid0(b):
                    dve.wait_ge(hid0_hi.sem, hid0_hi.at(me, b + 1))
                    low(hid0l[:, 2 * b:2 * b + 2, :], raw[:, b % 2, :, :], hid0h[:, 2 * b:2 * b + 2, :]).then_inc(hid0_lo.sem, 1)

                def conv(j):
                    for d in range(DB):
                        if j == 1:
                            dve.wait_ge(tap0.sem, tap0.at(me, d + 1))
                        else:
                            dve.wait_ge(conv_d.sem, conv_d.at(me, (j - 2) * DB + d + 1))
                        dve.scalar_tensor_tensor(shift[:, d, :], xbuf[:, d, j:j + N], convw_s[:, d, j:j + 1], shift[:, d, :],
                                                 ALU.mult, ALU.add).then_inc(conv_d.sem, 1)

                layer1(0)
                layer1(1)
                conv(1)
                layer1(2)
                layer1(3)
                conv(2)
                hid0(0)
                layer1(4)
                layer1(5)
                hid0(1)
                conv(3)
                layer1(6)
                layer1(7)
                hid0(2)
                dve.wait_ge(shift_hi.sem, shift_hi.at(me))
                low(partl[:], shift[:], parth[:]).then_inc(shift_lo.sem, 1)
                hid0(3)
                for c in range(NC):
                    dve.wait_ge(tanh_d.sem, tanh_d.at(me, c + 1))
                    dve.wait_ge(xt_mm.sem, xt_mm.at(me, c + 1))
                    dve.scalar_tensor_tensor(v[:, c, :], tanhv[:, c, :], 1.0, ab[c][:], ALU.add, ALU.mult).then_inc(v_d.sem, 1)
                if p == HALVES - 1:
                    dve.memset(xbuf[:, :, 0:W - 1], 0.0).then_inc(halo_d.sem, 1)
                else:
                    dve.tensor_copy(xbuf[:, :, 0:W - 1], xbuf[:, :, N:N + W - 1]).then_inc(halo_d.sem, 1)

                step = [0]

                def done(ins):
                    step[0] += 1
                    ins.then_inc(gs.sem, 1)

                def need(k):
                    dve.wait_ge(gs.sem, gs.at(me, k))

                dve.wait_ge(pr_mm.sem, pr_mm.at(me))
                dve.wait_ge(qk_ev.sem, qk_ev.at(me, 1))
                zg = ab[2][0:K, N:2 * N]
                done(dve.tensor_scalar(t1, zg, projb_s[0:K, :], 0.0, ALU.add, ALU.max))
                done(dve.tensor_scalar(t2, zg, projb_s[0:K, :], 0.0, ALU.add, ALU.min))
                need(2)
                done(dve.tensor_tensor(t4, t2, t1, ALU.subtract))
                dve.wait_ge(exp_d.sem, exp_d.at(me, 1))
                done(dve.tensor_scalar(bsum, t4, poly[LOG_DEG], None, ALU.mult))
                for i in range(LOG_DEG - 1, 0, -1):
                    need(step[0])
                    done(dve.scalar_tensor_tensor(bsum, bsum, poly[i], t4, ALU.add, ALU.mult))
                need(step[0])
                dve.wait_ge(exp_d.sem, exp_d.at(me, 2))
                done(dve.scalar_tensor_tensor(t5, bsum, poly[0], t5, ALU.add, ALU.mult))
                done(dve.scalar_tensor_tensor(t4, bsum, poly[0], t4, ALU.add, ALU.mult))
                need(step[0])
                done(dve.tensor_tensor(bsum, t4, t1, ALU.add))
                done(dve.tensor_tensor(t5, t5, t1, ALU.add))
                done(dve.tensor_scalar(t3, t3, 1.0, 0.5, ALU.add, ALU.mult))
                need(step[0])
                done(dve.tensor_tensor(t1, bsum, t3, ALU.mult))
                dve.wait_ge(ln_d.sem, ln_d.at(me))
                done(dve.tensor_tensor(t2, t5, t2, ALU.add))
                need(step[0])
                done(dve.tensor_tensor(t2, t2, t3, ALU.mult))
                done(dve.tensor_tensor_scan(bsum, restart_s[:], t1, 0.0, ALU.mult, ALU.add))
                need(step[0])
                for c in range(NC):
                    e = (c + 1) * CH - 1
                    neg = dve.tensor_scalar(nbt[:, c:c + 1], bsum[:, e:e + 1], -1.0, None, ALU.mult)
                done(neg)
                for i in range(LEVELS):
                    m = CH >> (i + 1)
                    bl, ll = levels(bsum, m), levels(lev[:, i, :], m)
                    mid = bl[:, :, 0, m - 1:m].to_broadcast([K, N // (2 * m), m])
                    dve.tensor_tensor(ll[:, :, 0, :], mid, bl[:, :, 0, :], ALU.subtract)
                    arg = dve.tensor_tensor(ll[:, :, 1, :], bl[:, :, 1, :], mid, ALU.subtract)
                arg.then_inc(levarg_d.sem, 1)
                dve.wait_ge(it_d.sem, it_d.at(me))
                dve.wait_ge(qk_ev.sem, qk_ev.at(me, 3))
                done(dve.tensor_tensor(k_s, k_s, t2, ALU.mult))
                need(step[0])
                assert step[0] == gs.n
                dve.wait_ge(dec_d.sem, dec_d.at(me))
                dve.tensor_tensor(t5, k_s, t5, ALU.mult).then_inc(kd_d.sem, 1)
                dve.tensor_tensor(t1, q_s, t1, ALU.mult).then_inc(qd_d.sem, 1)
                dve.wait_ge(lev_d.sem, lev_d.at(me))
                for i in range(LEVELS):
                    m = CH >> (i + 1)
                    lq = dve.tensor_tensor(levq[:, i, :].rearrange("p (b r) -> p b r", r=m), levels(lev[:, i, :], m)[:, :, 1, :],
                                           levels(q_s, m)[:, :, 1, :], ALU.mult)
                lq.then_inc(levq_d.sem, 1)
                dve.wait_ge(levq_d.sem, levq_d.at(me))
                dve.tensor_tensor(lev[:], lev[:], k_s.unsqueeze(1).to_broadcast([K, LEVELS, N]), ALU.mult).then_inc(levk_d.sem, 1)
                dve.wait_ge(dg_mm.sem, dg_mm.at(me))
                dve.tensor_scalar(ssk[:], ab[3][:, N:N + NC], KEPS2, None, ALU.max).then_inc(ss_d.sem, 1)
                dve.wait_ge(rkn_d.sem, rkn_d.at(me))
                for c in range(NC):
                    dve.scalar_tensor_tensor(att[:, c, :], ab[3][:, c * CH:(c + 1) * CH], rkn[:, c:c + 1], ident_s[:],
                                             ALU.mult, ALU.mult).then_inc(att_d.sem, 1)
                for c in range(NC):
                    dve.wait_ge(lv_mm.sem, lv_mm.at(me, c + 1))
                    dve.scalar_tensor_tensor(mprod[:, c, :, :].rearrange("p l u -> p (l u)"), ab[c][:, 0:LEVELS * UP], rkn[:, c:c + 1],
                                             masks_s[:].rearrange("p l u -> p (l u)"), ALU.mult, ALU.mult).then_inc(mask_d.sem, 1)
                dve.wait_ge(mask_d.sem, mask_d.at(me))
                for i in range(LEVELS):
                    m = CH >> (i + 1)
                    dve.wait_ge(att_d.sem, att_d.at(me, NC + i))
                    upper = att[:].rearrange("p c (b u r) -> p c b u r", u=2, r=m)[:, :, :, 1, :]
                    dve.tensor_tensor(upper, upper, mprod[:, :, i, :].rearrange("p c (b r) -> p c b r", r=m), ALU.add).then_inc(att_d.sem, 1)

                def hidden_low(dst, hi, b, done_hi, done_lo):
                    dve.wait_ge(done_hi.sem, done_hi.at(me, b + 1))
                    low(dst[:, 2 * b:2 * b + 2, :], raw[:, b % 2, :, :], hi[:, 2 * b:2 * b + 2, :]).then_inc(done_lo.sem, 1)

                for b in range(4):
                    hidden_low(hid1l, hid1h, b, hid1_hi, hid1_lo)
                if not (last and p == HALVES - 1):
                    statistics(me)
                    dve.wait_ge(stat_d.sem, stat_d.at(me, 2))

                def outputs(c):
                    t = slice(c * CH, (c + 1) * CH)
                    dve.wait_ge(ot_mm.sem, ot_mm.at(me, c + 1))
                    for d in range(DB):
                        o = dve.scalar_tensor_tensor(shift[:, d, t], shift[:, d, t], resw_s[:, d:d + 1], ab[c][:, d * CH:(d + 1) * CH],
                                                     ALU.mult, ALU.add)
                    o.then_inc(o_d.sem, 1)
                    dve.wait_ge(su_mm.sem, su_mm.at(me, c + 1))
                    new = ab[3 - c][0:K, :]
                    if p == 0 and c == 0:
                        dve.tensor_copy(state[:], new).then_inc(st_d.sem, 1)
                    else:
                        dve.wait_ge(st_d.sem, st_d.at(me, 1) if c else st_d.at(prev, 2))
                        dve.scalar_tensor_tensor(state[:], state[:], decay[:, c:c + 1], new, ALU.mult, ALU.add).then_inc(st_d.sem, 1)

                outputs(0)
                if not (last and p == HALVES - 1):
                    variances(me)
                    normalise(me)
                hidden_low(hid0l, hid0h, 0, hid2_hi, hid2_lo)
                outputs(1)
                dve.wait_ge(o_d.sem, o_d.at(me))
                dve.tensor_tensor(sgate[:], sgate[:], shift[:], ALU.mult).then_inc(xg_d.sem, 1)
                hidden_low(hid0l, hid0h, 1, hid2_hi, hid2_lo)
                dve.wait_ge(xg_hi.sem, xg_hi.at(me))
                low(partl[:], sgate[:], parth[:]).then_inc(xg_lo.sem, 1)
                for b in (2, 3):
                    hidden_low(hid0l, hid0h, b, hid2_hi, hid2_lo)
                if not (last and p == HALVES - 1):
                    ln_low(me)
                dve.wait_ge(rs_mm.sem, rs_mm.at(me))
                dve.tensor_scalar(msq[:], fb[1][:, 0:NC], 1.0 / DI, EPS, ALU.mult, ALU.add).then_inc(msq_d.sem, 1)
                dve.wait_ge(dn_mm.sem, dn_mm.at(me))
                dve.wait_ge(rms_d.sem, rms_d.at(me))
                for c in range(NC):
                    dve.scalar_tensor_tensor(xin[:, p, c, :], ab[3][:, c * H:(c + 1) * H], rms[:, c:c + 1], xin[:, p, c, :],
                                             ALU.mult, ALU.add).then_inc(fin_d.sem, 1)
                dve.wait_ge(w3_mm.sem, w3_mm.at(me))
                dve.tensor_tensor(ffn[:], fb[0][:].rearrange("p (c h) -> p c h", c=NC), s3_s[:].unsqueeze(1).to_broadcast([P, NC, H]),
                                  ALU.mult).then_inc(fin_d.sem, 1)
                dve.wait_ge(fin_d.sem, fin_d.at(me, 3))
                dve.tensor_tensor(xin[:, p, :, :], xin[:, p, :, :], ffn[:], ALU.add).then_inc(fin_d.sem, 1)

            dve.wait_ge(prep_act, len(CHUNKS))
            with dve.Fori(0, B - 1) as seq:
                for p in range(HALVES):
                    half(seq, p, False)
            for p in range(HALVES):
                half(B - 1, p, True)


def kernel(**inputs):
    import numpy as _np
    import concourse.bacc as _bacc
    from concourse import mybir as _mybir
    from concourse.bass_utils import run_bass_kernel_spmd as _run

    a = {n.removeprefix("L0_"): _np.asarray(v) for n, v in inputs.items()}

    def blocks(w):
        t = w.T.reshape(-1, P, w.shape[0])
        return t.transpose(1, 0, 2).reshape(P, -1)

    def columns(s):
        return s.reshape(-1, P).T

    up, w3 = a["attn_up_w"], blocks(a["ffn_w3_w"])
    chunk = {"comb": up.reshape(DB, P, H).transpose(1, 0, 2).reshape(P, -1), "up": blocks(up), "gate": blocks(a["attn_gate_w"]),
             "proj": _np.concatenate([blocks(_np.concatenate([a["attn_q_w"], a["attn_k_w"]])),
                                      blocks(_np.concatenate([a["attn_g_w"], a["attn_tau_w"]]))], axis=1),
             "down": blocks(a["attn_down_w"]), "w30": w3[:, :STAGE], "w31": w3[:, STAGE:]}
    for name in ("w1", "w2", "h1", "h2"):
        t = blocks(a[f"ffn_{name}_w"])
        for k in range(t.shape[1] // STAGE):
            chunk[f"{name}{k}"] = t[:, k * STAGE:(k + 1) * STAGE]
    token = _np.arange(CH)
    masks = _np.zeros((P, LEVELS, UP), _np.float32)
    for i in range(LEVELS):
        m = CH >> (i + 1)
        upper = token[token // m % 2 == 1]
        masks[:, i, :] = (token[:, None] // m % 2 == 0) & (token[:, None] // (2 * m) == upper[None, :] // (2 * m))
    arrays = {
        "x": a["attn_hidden_states"].reshape(B, HALVES, NC, P, H),
        "stage_w": _np.stack([chunk[n] for n in CHUNKS]),
        "ig1t": a["attn_ig_w1"].T.reshape(DB, P, R).transpose(1, 0, 2),
        "ig2t": _np.concatenate([a["attn_ig_w2"].T, a["attn_ig_b2"][None]]),
        "convw": a["attn_conv_w"].reshape(DB, P, W).transpose(1, 0, 2),
        "convb": columns(a["attn_conv_b"]),
        "projb": _np.concatenate([a["attn_g_b"], a["attn_tau_b"]])[:, None],
        "resw": columns(a["attn_residual_weight"]),
        "normw": columns(a["attn_norm_weight"]),
        "s1": columns(a["ffn_w1_s"]), "s2": columns(a["ffn_w2_s"]),
        "sh1": columns(a["ffn_h1_s"]), "sh2": columns(a["ffn_h2_s"]),
        "s3": _np.broadcast_to(a["ffn_w3_s"], (P, H)),
        "ident": _np.eye(P, dtype=_np.float32),
        "masks": masks,
        "restart": _np.broadcast_to((_np.arange(N) % CH != 0).astype(_np.float32), (K, N)),
    }
    nc = _bacc.Bacc("TRN2", target_bir_lowering=False, num_devices=1, dynamic_dma_scratch_size=1024)
    args = []
    for name, v in arrays.items():
        arrays[name] = v = _np.ascontiguousarray(v)
        args.append(nc.dram_tensor(name, v.shape, _mybir.dt.from_np(v.dtype), kind="ExternalInput").ap())
    args[0] = args[0].rearrange("b h c p d -> (b h) p c d")
    out = nc.dram_tensor("out", (B, HALVES, NC, P, H), F32, kind="ExternalOutput").ap()
    layer_program(nc, *args, out.rearrange("b h c p d -> (b h) p c d"))
    r = _run(nc, [arrays], core_ids=[0])
    return r.results[0]["out"].reshape(B, T, H)
```

```python
from contextlib import ExitStack

import concourse.bass as bass
import numpy as np
from concourse import mybir

F32 = mybir.dt.float32
F32R = mybir.dt.float32r
ALU = mybir.AluOpType
ACT = mybir.ActivationFunctionType

P = 128
B, T, H = 16, 512, 256
DI, K, R, W = 512, 64, 16, 4
F = 1024
CH = 128
NC = 2
N = CH * NC
HALVES = T // N
HB, DB, FB = H // P, DI // P, F // P
LEVELS = 7
UP = CH // 2
EPS = 1e-5
KEPS2 = 1e-24
STAGE = 1024
SLOTS = 4
LOG_DEG = 10

CHUNKS = (["comb", "up"] + [f"w1{k}" for k in range(2)] + [f"w2{k}" for k in range(2)] + ["gate", "proj"]
          + [f"h1{k}" for k in range(8)] + [f"h2{k}" for k in range(8)] + ["down", "w30", "w31"])
SPLIT = {"up": 0, "gate": 1, "proj": 2, "down": 3}
WHOLE = {n: i for i, n in enumerate(c for c in CHUNKS if c not in SPLIT and c != "comb")}


def log1p_ratio():
    e = (np.cos(np.pi * (np.arange(400) + 0.5) / 400) + 1) / 2
    c = np.polynomial.Chebyshev.fit(e, np.log1p(e) / e, LOG_DEG, domain=[0, 1])
    return [float(x) for x in c.convert(kind=np.polynomial.Polynomial).coef]


class Signal:

    def __init__(self, sem, per_half, primed=0):
        self.sem, self.n, self.primed = sem, per_half, primed

    def at(self, half, k=None):
        seq, place = half
        k = self.n if k is None else k
        return seq * (HALVES * self.n) + (place * self.n + k + self.primed)


def layer_program(nc, x, stage_w, ig1t, ig2t, convw, convb, projb, resw, normw, s1, s2, sh1, sh2, s3, ident,
                  masks, out):
    ctx = ExitStack()
    with ctx:
        def sb(name, shape, dt=F32):
            return ctx.enter_context(nc.sbuf_tensor(name, shape, dt))

        def sig(name, per_half, primed=0):
            return Signal(ctx.enter_context(nc.semaphore(name)), per_half, primed)

        def sem(name):
            return ctx.enter_context(nc.semaphore(name))

        wwhole = sb("wwhole", [P, len(WHOLE), STAGE], F32R)
        whi = sb("whi", [P, len(SPLIT), STAGE], F32R)
        wlo = sb("wlo", [P, len(SPLIT), STAGE], F32R)
        combh = sb("combh", [P, HB, R], F32R)
        combl = sb("combl", [P, HB, R], F32R)
        combw = sb("combw", [P, HB, R])
        ig1w = sb("ig1w", [P, DB, R])
        ig2w = sb("ig2w", [R + 1, DI])
        convw_s = sb("convw_s", [P, DB, W])
        convb_s = sb("convb_s", [P, DB])
        projb_s = sb("projb_s", [P, 1])
        projb_half = sb("projb_half", [P, 1])
        resw_s = sb("resw_s", [P, DB])
        normw_s = sb("normw_s", [P, DB])
        s1_s, s2_s = sb("s1_s", [P, FB]), sb("s2_s", [P, FB])
        sh1_s, sh2_s = sb("sh1_s", [P, FB]), sb("sh2_s", [P, FB])
        s3_s = sb("s3_s", [P, H])
        ident_s = sb("ident_s", [P, P])
        masks_s = sb("masks_s", [P, LEVELS, UP])
        ones = sb("ones", [P, CH])
        pair_ones = sb("pair_ones", [P, NC])
        minus_half = sb("minus_half", [P, NC])

        xin = sb("xin", [P, HALVES, NC, H])
        xnth, xntl = sb("xnth", [P, HB, N], F32R), sb("xntl", [P, HB, N], F32R)
        hid0h, hid0l = sb("hid0h", [P, FB, N], F32R), sb("hid0l", [P, FB, N], F32R)
        hid1h, hid1l = sb("hid1h", [P, FB, N], F32R), sb("hid1l", [P, FB, N], F32R)
        mixed = sb("mixed", [P, 4 * N])
        silu1 = mixed[:].rearrange("p (a t) -> p a t", a=4)
        mprod = mixed[:, 0:NC * LEVELS * UP].rearrange("p (c l u) -> p c l u", c=NC, l=LEVELS)
        ffn = mixed[:, 0:NC * H].rearrange("p (c h) -> p c h", c=NC)
        raw = sb("raw", [P, 2, 2, N])
        xbuf = sb("xbuf", [P, DB, W - 1 + N])
        shift = sb("shift", [P, DB, N])
        parth, partl = sb("parth", [P, DB, N], F32R), sb("partl", [P, DB, N], F32R)
        sgate = sb("sgate", [P, DB, N])
        zb = sb("zb", [R + 1, N])
        v = sb("v", [P, NC, DI])
        small = sb("small", [P, 8, CH])
        work = sb("work", [P, DB * N + NC * H + N])
        tanhv = work[:, 0:NC * DI].rearrange("p (c d) -> p c d", c=NC)
        lev = work[:, 0:LEVELS * CH].rearrange("p (l t) -> p l t", l=LEVELS)
        levq = work[:, LEVELS * CH:LEVELS * (CH + UP)].rearrange("p (l t) -> p l t", l=LEVELS)
        sq = work[:, 0:DB * N].rearrange("p (d t) -> p d t", d=DB)
        xn = work[:, DB * N:DB * N + NC * H].rearrange("p (c h) -> p c h", c=NC)
        sqsum = work[:, DB * N + NC * H:]
        att = sb("att", [P, NC, CH])
        state = sb("state", [P, DI])
        kdt = sb("kdt", [P, NC, K])
        stats = sb("stats", [P, NC, 6])
        mv = sb("mv", [P, NC, 2])
        varp, rstd = sb("varp", [P, NC]), sb("rstd", [P, NC])
        ssk, rkn = sb("ssk", [P, NC]), sb("rkn", [P, NC])
        msq, rms = sb("msq", [P, NC]), sb("rms", [P, NC])
        nbt, decay = sb("nbt", [P, 1]), sb("decay", [P, 1])

        fb = [ctx.enter_context(nc.psum_tensor(f"fb{i}", [P, 512], F32)) for i in range(4)]
        ab = [ctx.enter_context(nc.psum_tensor(f"ab{i}", [P, 512], F32)) for i in range(4)]

        const_in = sem("const_in")
        stage_in = [sem(f"stage_in{i}") for i in range(SLOTS)]
        prep_act, prep_dve, prep_pe, prep_pool = sem("prep_act"), sem("prep_dve"), sem("prep_pe"), sem("prep_pool")
        x_in = [sem(f"x_in{i}") for i in range(HALVES)]
        x_out = [sem(f"x_out{i}") for i in range(HALVES)]
        up_mm, z_mm, l1_mm, gate_mm = sig("up_mm", 2), sig("z_mm", 1), sig("l1_mm", FB), sig("gate_mm", 2)
        xt_mm, ig_mm, pr_mm, dg_mm = sig("xt_mm", NC), sig("ig_mm", NC), sig("pr_mm", 1), sig("dg_mm", 1)
        lv_mm, kt_mm, ot_mm, su_mm = sig("lv_mm", NC), sig("kt_mm", 1), sig("ot_mm", NC), sig("su_mm", NC)
        h1_mm, h2_mm, dn_mm = sig("h1_mm", 4), sig("h2_mm", 4), sig("dn_mm", 1)
        rs_mm, ln_mm, w3_mm = sig("rs_mm", 1), sig("ln_mm", 1, 1), sig("w3_mm", 1)
        x_ev, z_ev, tap0, silu_d = sig("x_ev", 2), sig("z_ev", 1), sig("tap0", DB), sig("silu_d", FB)
        hid0_hi, gate_ev, shift_d, shift_hi = sig("hid0_hi", 4), sig("gate_ev", 2), sig("shift_d", 1), sig("shift_hi", 1)
        tanh_d, qk_ev, exp_d, ln_d, it_d = sig("tanh_d", NC), sig("qk_ev", 4 * NC), sig("exp_d", 2), sig("ln_d", 1), sig("it_d", 1)
        lev_d, dec_d, kd_ev = sig("lev_d", 1), sig("dec_d", 3), sig("kd_ev", NC)
        gelu1_d, hid1_hi, gelu2_d, hid2_hi = sig("gelu1_d", FB), sig("hid1_hi", 4), sig("gelu2_d", FB), sig("hid2_hi", 4)
        sq_d, xg_hi, ln_hi = sig("sq_d", 1), sig("xg_hi", 1), sig("ln_hi", 1, 1)
        conv_d, l1_d, hid0_lo, shift_lo = sig("conv_d", DB * (W - 1)), sig("l1_d", FB), sig("hid0_lo", 4), sig("shift_lo", 1)
        halo_d = sig("halo_d", 1, 1)
        v_d, gs = sig("v_d", NC), sig("gs", LOG_DEG + 14 + 2 * (NC - 1))
        levarg_d, levq_d, levk_d, kd_d, qd_d = sig("levarg_d", 1), sig("levq_d", 1), sig("levk_d", 1), sig("kd_d", 1), sig("qd_d", 1)
        ss_d, att_d, mask_d = sig("ss_d", 1), sig("att_d", LEVELS + 2), sig("mask_d", NC)
        st_d, o_d, xg_d, xg_lo = sig("st_d", NC), sig("o_d", NC, NC), sig("xg_d", 1), sig("xg_lo", 1)
        sqsum_d = sig("sqsum_d", 1)
        hid1_lo, hid2_lo = sig("hid1_lo", 4), sig("hid2_lo", 4)
        msq_d, fin_d, stat_d, var_d, xn_d, ln_lo = (sig("msq_d", 1, 1), sig("fin_d", 5, 5), sig("stat_d", 3, 3),
                                                    sig("var_d", 1, 1), sig("xn_d", 1, 1), sig("ln_lo", 1, 1))
        rkn_d, rms_d, rstd_d = sig("rkn_d", 1), sig("rms_d", 1), sig("rstd_d", 1, 1)

        G_ABS = 2 * NC + 1
        G_POLY = G_ABS + LOG_DEG

        q_s, k_s, bsum, t1, t2, t3, t4, t5 = (small[:, i, :] for i in range(8))
        CONSTS = [(ig1w, ig1t), (ig2w, ig2t), (convw_s, convw), (convb_s, convb), (projb_s, projb), (resw_s, resw),
                  (normw_s, normw), (s1_s, s1), (s2_s, s2), (sh1_s, sh1), (sh2_s, sh2), (s3_s, s3), (ident_s, ident),
                  (masks_s, masks)]

        def ready(names):
            return max(CHUNKS.index(n) for n in names) + 1

        def stage_slot(n):
            return (sgate[:].rearrange("p d t -> p (d t)"), shift[:].rearrange("p d t -> p (d t)"),
                    v[:].rearrange("p c d -> p (c d)"), raw[:].rearrange("p a b t -> p (a b t)"))[n % SLOTS]

        def rows(c):
            return slice(c * K, (c + 1) * K)

        def own(c):
            return ab[3 - c][:, P:P + CH]

        def levels(ap, m):
            return ap.rearrange("p (b u r) -> p b u r", u=2, r=m)

        block = ctx.enter_context(nc.Block())

        @block.sync
        def _(sp):
            sp.sem_inc(x_out[1], 16)
            sp.dma_start(xin[:, 0, :, :], x[0]).then_inc(x_in[0], 16)
            for dst, src in CONSTS:
                sp.dma_start(dst[:], src).then_inc(const_in, 16)
            for n in range(len(CHUNKS)):
                if n >= SLOTS:
                    sp.wait_ge(prep_act, n - SLOTS + 1)
                    sp.wait_ge(prep_dve, n - SLOTS + 1)
                sp.dma_start(stage_slot(n), stage_w[n]).then_inc(stage_in[n % SLOTS], 16)

            def half(seq, p, last):
                me = (seq, p)
                if not (last and p == HALVES - 1):
                    if p == 0:
                        sp.wait_ge(x_out[1], seq * 16 + 16)
                        sp.dma_start(xin[:, 1, :, :], x[seq * HALVES + 1]).then_inc(x_in[1], 16)
                    else:
                        sp.wait_ge(x_out[0], seq * 16 + 16)
                        sp.dma_start(xin[:, 0, :, :], x[seq * HALVES + HALVES]).then_inc(x_in[0], 16)
                sp.wait_ge(fin_d.sem, fin_d.at(me))
                sp.dma_start(out[seq * HALVES + p], xin[:, p, :, :]).then_inc(x_out[p], 16)

            with sp.Fori(0, B - 1) as seq:
                for p in range(HALVES):
                    half(seq, p, False)
            for p in range(HALVES):
                half(B - 1, p, True)
            sp.wait_ge(x_out[0], B * 16)
            sp.wait_ge(x_out[1], B * 16 + 16)

        @block.gpsimd
        def _(pool):
            pool.memset(minus_half[:], -0.5).then_inc(prep_pool, 1)
            pool.memset(ones[:], 1.0).then_inc(prep_pool, 1)
            pool.memset(zb[:], 1.0).then_inc(prep_pool, 1)
            pool.memset(xbuf[:], 0.0).then_inc(prep_pool, 1)
            pool.wait_ge(prep_pool, 1)

            def normalise(me):
                pool.wait_ge(var_d.sem, var_d.at(me))
                pool.tensor_tensor(rstd[:], varp[:], minus_half[:], ALU.pow).then_inc(rstd_d.sem, 1)

            def half(seq, p, last):
                me = (seq, p)
                pool.wait_ge(ss_d.sem, ss_d.at(me))
                pool.tensor_tensor(rkn[:], ssk[:], minus_half[:], ALU.pow).then_inc(rkn_d.sem, 1)
                if not (last and p == HALVES - 1):
                    normalise(me)
                pool.wait_ge(msq_d.sem, msq_d.at(me))
                pool.tensor_tensor(rms[:], msq[:], minus_half[:], ALU.pow).then_inc(rms_d.sem, 1)

            normalise((0, -1))
            with pool.Fori(0, B - 1) as seq:
                for p in range(HALVES):
                    half(seq, p, False)
            for p in range(HALVES):
                half(B - 1, p, True)

        @block.tensor
        def _(pe):
            def wide(o, pairs, start=True, stop=True):
                for i, (a, b) in enumerate(pairs):
                    mm = pe.matmul(o, a, b, start=start and i == 0, stop=stop and i == len(pairs) - 1)
                return mm

            def three(whi_b, wlo_b, ah, al):
                return [(whi_b, ah), (whi_b, al), (wlo_b, ah)]

            def split_w(name, k, lo, hi, width):
                i = SPLIT[name]
                return whi[:, i, k * width + lo:k * width + hi], wlo[:, i, k * width + lo:k * width + hi]

            def fw(name, k, lo, hi):
                return wwhole[:, WHOLE[f"{name}{k}"], lo:hi]

            pe.wait_ge(const_in, 16 * len(CONSTS))
            pe.wait_ge(stage_in[0], 16)
            for h in range(HB):
                for d in range(DB):
                    mm = pe.matmul(ab[0][:, h * R:(h + 1) * R], stage_slot(0)[:, d * H + h * P:d * H + (h + 1) * P],
                                   ig1w[:, d, :], start=(d == 0), stop=(d == DB - 1))
            mm.then_inc(prep_pe, 1)

            def ln_transpose(me, first=False):
                pe.wait_ge(xn_d.sem, xn_d.at(me))
                if not first:
                    pe.wait_ge(st_d.sem, st_d.at(me, 2))
                for h in range(HB):
                    for c in range(NC):
                        mm = pe.transpose(ab[2][:, h * N + c * CH:h * N + (c + 1) * CH], xn[:, c, h * P:(h + 1) * P], ident_s[:])
                mm.then_inc(ln_mm.sem, 1)

            ln_transpose((0, -1), True)

            def half(seq, p, last):
                me, prev = (seq, p), (seq, p - 1)
                xh, xl = xnth, xntl
                pe.wait_ge(ln_hi.sem, ln_hi.at(prev))
                pe.wait_ge(ln_lo.sem, ln_lo.at(prev))
                pe.wait_ge(prep_act, ready(["up"]))
                pe.wait_ge(prep_dve, ready(["up"]))
                for b in range(2):
                    pe.wait_ge(o_d.sem, o_d.at(prev, b + 1))
                    for m in (2 * b, 2 * b + 1):
                        pairs = []
                        for k in range(HB):
                            pairs += three(*split_w("up", k, m * P, (m + 1) * P, DI), xh[:, k, :], xl[:, k, :])
                        mm = wide(ab[b][:, (m % 2) * N:(m % 2 + 1) * N], pairs)
                    mm.then_inc(up_mm.sem, 1)
                pairs = []
                for k in range(HB):
                    pairs += three(combh[:, k, :], combl[:, k, :], xh[:, k, :], xl[:, k, :])
                wide(ab[2][0:R, 0:N], pairs).then_inc(z_mm.sem, 1)

                def layer1(m):
                    if m in (0, 2):
                        pe.wait_ge(fin_d.sem, fin_d.at(prev, m // 2 + 1))
                    elif m == 1:
                        pe.wait_ge(msq_d.sem, msq_d.at(prev))
                    elif m >= 4:
                        pe.wait_ge(l1_d.sem, l1_d.at(me, m - 3))
                    for j, w in enumerate(("w1", "w2")):
                        pairs = []
                        for k in range(HB):
                            wb = fw(w, k, m * P, (m + 1) * P)
                            pairs += [(wb, xh[:, k, :]), (wb, xl[:, k, :])]
                        mm = wide(fb[m % 4][:, j * N:(j + 1) * N], pairs)
                    mm.then_inc(l1_mm.sem, 1)

                def gate(b):
                    if b == 0:
                        pe.wait_ge(z_ev.sem, z_ev.at(me))
                    else:
                        pe.wait_ge(fin_d.sem, fin_d.at(prev))
                    for m in (2 * b, 2 * b + 1):
                        pairs = []
                        for k in range(HB):
                            pairs += three(*split_w("gate", k, m * P, (m + 1) * P, DI), xh[:, k, :], xl[:, k, :])
                        mm = wide(ab[2 + b][:, (m % 2) * N:(m % 2 + 1) * N], pairs)
                    mm.then_inc(gate_mm.sem, 1)

                pe.wait_ge(prep_act, ready(["w11", "w21"]))
                pe.wait_ge(prep_dve, ready(["w11", "w21"]))
                for m in range(4):
                    layer1(m)
                pe.wait_ge(prep_act, ready(["proj"]))
                pe.wait_ge(prep_dve, ready(["proj"]))
                gate(0)
                gate(1)
                for m in range(4, FB):
                    layer1(m)
                for c in range(NC):
                    pe.wait_ge(x_ev.sem, x_ev.at(me))
                    for d in range(DB):
                        mm = pe.transpose(ab[c][:, d * P:(d + 1) * P], xbuf[:, d, W - 1 + c * CH:W - 1 + (c + 1) * CH], ident_s[:])
                    mm.then_inc(xt_mm.sem, 1)
                for c in range(NC):
                    pe.wait_ge(gate_ev.sem, gate_ev.at(me, c + 1))
                    pe.matmul(ab[2 + c][:], zb[:, c * CH:(c + 1) * CH], ig2w[:], start=True, stop=True).then_inc(ig_mm.sem, 1)
                pe.wait_ge(shift_hi.sem, shift_hi.at(me))
                pe.wait_ge(shift_lo.sem, shift_lo.at(me))
                pe.wait_ge(tanh_d.sem, tanh_d.at(me, 1))
                for j in range(2):
                    pairs = []
                    for k in range(DB):
                        lo = j * DI + k * P
                        pairs += three(whi[:, SPLIT["proj"], lo:lo + P], wlo[:, SPLIT["proj"], lo:lo + P], parth[:, k, :], partl[:, k, :])
                    mm = wide(ab[2][:, j * N:(j + 1) * N], pairs)
                mm.then_inc(pr_mm.sem, 1)
                pe.wait_ge(hid0_hi.sem, hid0_hi.at(me))
                pe.wait_ge(hid0_lo.sem, hid0_lo.at(me))
                pe.wait_ge(prep_act, ready(["h17"]))
                pe.wait_ge(prep_dve, ready(["h17"]))

                def hidden(name, b, ih, il, done):
                    for m in (2 * b, 2 * b + 1):
                        pairs = []
                        for k in range(FB):
                            wb = fw(name, k, m * P, (m + 1) * P)
                            pairs += [(wb, ih[:, k, :]), (wb, il[:, k, :])]
                        mm = wide(fb[b][:, (m % 2) * N:(m % 2 + 1) * N], pairs)
                    mm.then_inc(done.sem, 1)

                for b in range(4):
                    pe.wait_ge(l1_d.sem, l1_d.at(me, b + 5))
                    hidden("h1", b, hid0h, hid0l, h1_mm)
                pe.wait_ge(gs.sem, gs.at(me))
                pe.wait_ge(qk_ev.sem, qk_ev.at(me))
                pe.wait_ge(tanh_d.sem, tanh_d.at(me, 2))
                pe.wait_ge(kd_d.sem, kd_d.at(me))
                pe.transpose(ab[2][:, 0:P], t5, ident_s[:]).then_inc(kt_mm.sem, 1)
                pe.matmul(ab[3][:, N:N + NC], t4, pair_ones[:], start=True, stop=True)
                for c in range(NC):
                    mm = pe.matmul(own(c), k_s[rows(c), :], q_s[rows(c), :], start=True, stop=True)
                mm.then_inc(dg_mm.sem, 1)
                for c in range(NC):
                    pe.wait_ge(v_d.sem, v_d.at(me, c + 1))
                    pe.wait_ge(levq_d.sem, levq_d.at(me))
                    pe.wait_ge(levk_d.sem, levk_d.at(me))
                    for i in range(LEVELS):
                        mm = pe.matmul(ab[c][:, i * UP:(i + 1) * UP], lev[rows(c), i, :], levq[rows(c), i, :], start=True, stop=True)
                    mm.then_inc(lv_mm.sem, 1)

                def outputs(c):
                    pe.wait_ge(mask_d.sem, mask_d.at(me, c + 1))
                    pe.wait_ge(att_d.sem, att_d.at(me))
                    carried = not (p == 0 and c == 0)
                    if carried:
                        pe.wait_ge(st_d.sem, st_d.at(me, 1) if c else st_d.at(prev, 2))
                        pe.wait_ge(qd_d.sem, qd_d.at(me))
                    for d in range(DB):
                        mm = pe.matmul(ab[c][:, d * CH:(d + 1) * CH], v[:, c, d * P:(d + 1) * P], att[:, c, :],
                                       start=True, stop=not carried)
                        if carried:
                            mm = pe.matmul(ab[c][:, d * CH:(d + 1) * CH], state[rows(c), d * P:(d + 1) * P], t1[rows(c), :],
                                           start=False, stop=True)
                    mm.then_inc(ot_mm.sem, 1)
                    pe.wait_ge(kd_ev.sem, kd_ev.at(me))
                    pe.matmul(ab[3 - c][rows(c), :], kdt[:, c, :], v[:, c, :], start=True, stop=True).then_inc(su_mm.sem, 1)

                pe.wait_ge(prep_act, ready(["h27"]))
                pe.wait_ge(prep_dve, ready(["h27"]))
                for b in range(4):
                    pe.wait_ge(gelu1_d.sem, gelu1_d.at(me, 2 * b + 2))
                    if b == 0:
                        pe.wait_ge(hid1_hi.sem, hid1_hi.at(me))
                        pe.wait_ge(hid1_lo.sem, hid1_lo.at(me))
                    hidden("h2", b, hid1h, hid1l, h2_mm)
                    if b in (1, 2):
                        outputs(b - 1)
                if not (last and p == HALVES - 1):
                    ln_transpose(me)
                pe.wait_ge(prep_act, ready(["w31"]))
                pe.wait_ge(prep_dve, ready(["w31"]))
                for ks, b in ((range(FB - 2), 3), (range(FB - 2, FB), 4)):
                    pe.wait_ge(hid2_hi.sem, hid2_hi.at(me, b))
                    pe.wait_ge(hid2_lo.sem, hid2_lo.at(me, b))
                    for c in range(NC):
                        t = slice(c * CH, (c + 1) * CH)
                        pairs = []
                        for k in ks:
                            wb = fw("w3", k // 4, (k % 4) * H, (k % 4 + 1) * H)
                            pairs += [(hid0h[:, k, t], wb), (hid0l[:, k, t], wb)]
                        mm = wide(fb[2 * c][:, 0:H], pairs, start=(b == 3), stop=(b == 4))
                mm.then_inc(w3_mm.sem, 1)
                pe.wait_ge(xg_hi.sem, xg_hi.at(me))
                pe.wait_ge(xg_lo.sem, xg_lo.at(me))
                pe.wait_ge(st_d.sem, st_d.at(me, 1))
                for c in range(NC):
                    t = slice(c * CH, (c + 1) * CH)
                    pairs = []
                    for k in range(DB):
                        wh, wl = split_w("down", k, 0, H, H)
                        pairs += [(parth[:, k, t], wh), (partl[:, k, t], wh), (parth[:, k, t], wl)]
                    mm = wide(ab[3][:, c * H:(c + 1) * H], pairs)
                mm.then_inc(dn_mm.sem, 1)
                pe.wait_ge(sqsum_d.sem, sqsum_d.at(me))
                pe.wait_ge(gelu2_d.sem, gelu2_d.at(me, 4))
                for c in range(NC):
                    mm = pe.matmul(fb[1][:, c:c + 1], sqsum[:, c * CH:(c + 1) * CH], ones[:, 0:1], start=True, stop=True)
                mm.then_inc(rs_mm.sem, 1)

            pe.wait_ge(prep_pool, 4)
            with pe.Fori(0, B - 1) as seq:
                for p in range(HALVES):
                    half(seq, p, False)
            for p in range(HALVES):
                half(B - 1, p, True)

        @block.scalar
        def _(act):
            act.wait_ge(const_in, 16 * len(CONSTS))

            def ln_high(me):
                act.wait_ge(ln_mm.sem, ln_mm.at(me))
                if me[1] >= 0:
                    act.wait_ge(l1_mm.sem, l1_mm.at(me))
                act.activation(xnth[:], ab[2][:].rearrange("p (h t) -> p h t", h=HB), ACT.Copy).then_inc(ln_hi.sem, 1)

            for n, name in enumerate(CHUNKS):
                if name == "comb":
                    act.wait_ge(prep_pe, 1)
                    act.activation(combh[:], ab[0][:, 0:HB * R].rearrange("p (h r) -> p h r", h=HB), ACT.Copy).then_inc(prep_act, 1)
                    ln_high((0, -1))
                    continue
                act.wait_ge(stage_in[n % SLOTS], 16 * (n // SLOTS + 1))
                if name == "down":
                    for d in range(DB):
                        mul = act.activation(whi[:, SPLIT[name], d * H:(d + 1) * H], stage_slot(n)[:, d * H:(d + 1) * H], ACT.Copy,
                                             scale=normw_s[:, d:d + 1])
                    mul.then_inc(prep_act, 1)
                elif name in SPLIT:
                    act.activation(whi[:, SPLIT[name], :], stage_slot(n), ACT.Copy).then_inc(prep_act, 1)
                else:
                    act.activation(wwhole[:, WHOLE[name], 0:STAGE // 2], stage_slot(n)[:, 0:STAGE // 2], ACT.Copy).then_inc(prep_act, 1)

            def half(seq, p, last):
                me, prev = (seq, p), (seq, p - 1)

                for b in range(2):
                    act.wait_ge(up_mm.sem, up_mm.at(me, b + 1))
                    if b == 0:
                        act.wait_ge(halo_d.sem, halo_d.at(prev))
                    act.activation(xbuf[:, 2 * b:2 * b + 2, W - 1:], ab[b][:].rearrange("p (d t) -> p d t", d=2), ACT.Copy).then_inc(x_ev.sem, 1)
                act.wait_ge(z_mm.sem, z_mm.at(me))
                act.activation(zb[0:R, :], ab[2][0:R, 0:N], ACT.Copy).then_inc(z_ev.sem, 1)
                act.wait_ge(x_ev.sem, x_ev.at(me))
                for d in range(DB):
                    act.activation(shift[:, d, :], xbuf[:, d, 0:N], ACT.Identity, bias=convb_s[:, d:d + 1],
                                   scale=convw_s[:, d, 0:1]).then_inc(tap0.sem, 1)

                def high(src, dst, b, done):
                    act.activation(dst[:, 2 * b:2 * b + 2, :], src, ACT.Copy).then_inc(done.sem, 1)

                def silu(m):
                    if m == 0:
                        act.wait_ge(fin_d.sem, fin_d.at(prev, 3))
                    act.wait_ge(l1_mm.sem, l1_mm.at(me, m + 1))
                    if m >= 4:
                        act.wait_ge(l1_d.sem, l1_d.at(me, m - 3))
                    act.activation(silu1[:, m % 4, :], fb[m % 4][:, 0:N], ACT.Silu, scale=s1_s[:, m:m + 1]).then_inc(silu_d.sem, 1)

                def hid0(b):
                    act.wait_ge(l1_d.sem, l1_d.at(me, 2 * b + 2))
                    high(raw[:, b % 2, :, :], hid0h, b, hid0_hi)

                def gate(b):
                    act.wait_ge(gate_mm.sem, gate_mm.at(me, b + 1))
                    act.activation(sgate[:, 2 * b:2 * b + 2, :], ab[2 + b][:].rearrange("p (d t) -> p d t", d=2), ACT.Silu).then_inc(gate_ev.sem, 1)

                for m in range(4):
                    silu(m)
                gate(0)
                act.wait_ge(conv_d.sem, conv_d.at(me))
                act.activation(shift[:], shift[:], ACT.Silu).then_inc(shift_d.sem, 1)
                gate(1)
                act.wait_ge(shift_d.sem, shift_d.at(me))
                act.activation(parth[:], shift[:], ACT.Copy).then_inc(shift_hi.sem, 1)
                hid0(0)
                hid0(1)
                for m in range(4, FB):
                    silu(m)
                for c in range(NC):
                    if c == 1:
                        hid0(2)
                    act.wait_ge(ig_mm.sem, ig_mm.at(me, c + 1))
                    act.activation(tanhv[:, c, :], ab[2 + c][:], ACT.Tanh, scale=0.5).then_inc(tanh_d.sem, 1)
                hid0(3)
                act.wait_ge(pr_mm.sem, pr_mm.at(me))
                for c in range(NC):
                    act.activation(t3[rows(c), :], ab[2][K:P, N + c * CH:N + (c + 1) * CH], ACT.Tanh, bias=projb_half[K:P, :],
                                   scale=0.5).then_inc(qk_ev.sem, 1)
                act.preload_act_table_set("natural_log_exp_and_others")
                for c in range(NC):
                    act.activation(k_s[rows(c), :], ab[2][K:P, c * CH:(c + 1) * CH], ACT.Copy).then_inc(qk_ev.sem, 1)
                act.wait_ge(gs.sem, gs.at(me, 2 * NC))
                for c in range(NC):
                    act.activation(q_s[rows(c), :], ab[2][0:K, c * CH:(c + 1) * CH], ACT.Copy, scale=0.5 * K ** -0.5).then_inc(qk_ev.sem, 1)
                act.wait_ge(gs.sem, gs.at(me, G_ABS))
                act.activation(t4, t4, ACT.Exp).then_inc(exp_d.sem, 1)
                act.activation(t5, t1, ACT.Exp, scale=-1.0).then_inc(exp_d.sem, 1)
                act.wait_ge(gs.sem, gs.at(me, G_POLY + 4))
                act.activation(t5, t5, ACT.Ln).then_inc(ln_d.sem, 1)
                act.wait_ge(gs.sem, gs.at(me, G_POLY + 8))
                act.activation(t2, t2, ACT.Exp).then_inc(it_d.sem, 1)
                act.wait_ge(gs.sem, gs.at(me, G_POLY + 10))
                act.activation(t1, bsum, ACT.Exp, scale=-1.0).then_inc(dec_d.sem, 1)
                act.activation(t5, bsum, ACT.Exp, bias=nbt[:]).then_inc(dec_d.sem, 1)
                act.activation(decay[:], nbt[:], ACT.Exp).then_inc(dec_d.sem, 1)
                for c in range(NC):
                    act.activation(t4[rows(c), :], ab[2][K:P, c * CH:(c + 1) * CH], ACT.Square).then_inc(qk_ev.sem, 1)
                act.wait_ge(levarg_d.sem, levarg_d.at(me))
                act.activation(lev[:], lev[:], ACT.Exp, scale=-1.0).then_inc(lev_d.sem, 1)
                act.preload_act_table_set("gelu_and_others")
                def gelu(mm, scales, dst, b, done, done_hi, free):
                    act.wait_ge(mm.sem, mm.at(me, b + 1))
                    if free is not None:
                        act.wait_ge(*free)
                    for j in range(2):
                        act.activation(raw[:, b % 2, j, :], fb[b][:, j * N:(j + 1) * N], ACT.Gelu,
                                       scale=scales[:, 2 * b + j:2 * b + j + 1]).then_inc(done.sem, 1)
                    act.wait_ge(done.sem, done.at(me, 2 * b + 2))
                    high(raw[:, b % 2, :, :], dst, b, done_hi)

                for b in range(4):
                    lo = (hid0_lo, b + 3) if b < 2 else (hid1_lo, b - 1)
                    gelu(h1_mm, sh1_s, hid1h, b, gelu1_d, hid1_hi, (lo[0].sem, lo[0].at(me, lo[1])))
                act.wait_ge(rkn_d.sem, rkn_d.at(me))
                act.wait_ge(att_d.sem, att_d.at(me, NC))
                for c in range(NC):
                    act.activation(kdt[:, c, :], ab[2][:, c * K:(c + 1) * K], ACT.Copy, scale=rkn[:, c:c + 1]).then_inc(kd_ev.sem, 1)
                for b in range(4):
                    lo = (hid1_lo, b + 3) if b < 2 else (hid2_lo, b - 1)
                    gelu(h2_mm, sh2_s, hid0h, b, gelu2_d, hid2_hi, (lo[0].sem, lo[0].at(me, lo[1])))
                if not (last and p == HALVES - 1):
                    ln_high(me)
                act.wait_ge(xg_d.sem, xg_d.at(me))
                act.activation(parth[:], sgate[:], ACT.Copy).then_inc(xg_hi.sem, 1)
                act.activation(sq[:], sgate[:], ACT.Square).then_inc(sq_d.sem, 1)
                act.preload_act_table_set("silu_and_others")

            act.wait_ge(prep_dve, len(CHUNKS))
            with act.Fori(0, B - 1) as seq:
                for p in range(HALVES):
                    half(seq, p, False)
            for p in range(HALVES):
                half(B - 1, p, True)

        @block.vector
        def _(dve):
            poly = log1p_ratio()
            for s in (o_d, fin_d, msq_d, halo_d):
                dve.sem_inc(s.sem, s.primed)

            def low(dst, src, hi):
                return dve.tensor_tensor(dst, src, hi.bitcast(F32), ALU.subtract)

            def statistics(me):
                seq, p = me
                if p == -1:
                    nxt = 0
                    dve.wait_ge(x_in[0], 16)
                else:
                    nxt = 1 - p
                    dve.wait_ge(x_in[nxt], seq * 16 + (16 if p == 0 else 32))
                for c in range(NC):
                    dve.bn_stats(stats[:, c, :], xin[:, nxt, c, :]).then_inc(stat_d.sem, 1)

            def variances(me):
                for c in range(NC):
                    ag = dve.bn_aggr(mv[:, c, :], stats[:, c, :])
                ag.then_inc(stat_d.sem, 1)
                dve.wait_ge(stat_d.sem, stat_d.at(me, 3))
                dve.tensor_scalar(varp[:], mv[:, :, 1], EPS, None, ALU.add).then_inc(var_d.sem, 1)

            def normalise(me):
                seq, p = me
                nxt = 0 if p == -1 else 1 - p
                dve.wait_ge(rstd_d.sem, rstd_d.at(me))
                for c in range(NC):
                    ts = dve.tensor_scalar(xn[:, c, :], xin[:, nxt, c, :], mv[:, c, 0:1], rstd[:, c:c + 1], ALU.subtract, ALU.mult)
                ts.then_inc(xn_d.sem, 1)

            def ln_low(me):
                dve.wait_ge(ln_hi.sem, ln_hi.at(me))
                low(xntl[:], ab[2][:].rearrange("p (h t) -> p h t", h=HB), xnth[:]).then_inc(ln_lo.sem, 1)

            dve.wait_ge(const_in, 16 * len(CONSTS))
            for n, name in enumerate(CHUNKS):
                if name == "comb":
                    dve.wait_ge(prep_pe, 1)
                    dve.wait_ge(prep_act, 1)
                    for c in range(NC):
                        for col in range(NC):
                            dve.memset(pair_ones[rows(c), col:col + 1], float(c == col))
                    dve.tensor_scalar(projb_half[:], projb_s[:], 0.5, None, ALU.mult)
                    low(combl[:], ab[0][:, 0:HB * R].rearrange("p (h r) -> p h r", h=HB), combh[:]).then_inc(prep_dve, 1)
                    statistics((0, -1))
                    dve.wait_ge(stat_d.sem, stat_d.at((0, -1), 2))
                    variances((0, -1))
                    normalise((0, -1))
                    ln_low((0, -1))
                    continue
                dve.wait_ge(stage_in[n % SLOTS], 16 * (n // SLOTS + 1))
                if name in SPLIT:
                    dve.wait_ge(prep_act, n + 1)
                    if name == "down":
                        for d in range(DB):
                            t = slice(d * H, (d + 1) * H)
                            st = dve.scalar_tensor_tensor(wlo[:, SPLIT[name], t], stage_slot(n)[:, t], normw_s[:, d:d + 1],
                                                          whi[:, SPLIT[name], t].bitcast(F32), ALU.mult, ALU.subtract)
                        st.then_inc(prep_dve, 1)
                    else:
                        low(wlo[:, SPLIT[name], :], stage_slot(n), whi[:, SPLIT[name], :]).then_inc(prep_dve, 1)
                else:
                    dve.tensor_copy(wwhole[:, WHOLE[name], STAGE // 2:], stage_slot(n)[:, STAGE // 2:]).then_inc(prep_dve, 1)

            def half(seq, p, last):
                me, prev = (seq, p), (seq, p - 1)

                def layer1(m):
                    if m >= 4:
                        dve.wait_ge(hid0_lo.sem, hid0_lo.at(me, m // 2 - 1))
                    dve.wait_ge(silu_d.sem, silu_d.at(me, m + 1))
                    dve.scalar_tensor_tensor(raw[:, (m // 2) % 2, m % 2, :], fb[m % 4][:, N:2 * N], s2_s[:, m:m + 1],
                                             silu1[:, m % 4, :], ALU.mult, ALU.mult).then_inc(l1_d.sem, 1)

                def hid0(b):
                    dve.wait_ge(hid0_hi.sem, hid0_hi.at(me, b + 1))
                    low(hid0l[:, 2 * b:2 * b + 2, :], raw[:, b % 2, :, :], hid0h[:, 2 * b:2 * b + 2, :]).then_inc(hid0_lo.sem, 1)

                def conv(j):
                    for d in range(DB):
                        if j == 1:
                            dve.wait_ge(tap0.sem, tap0.at(me, d + 1))
                        else:
                            dve.wait_ge(conv_d.sem, conv_d.at(me, (j - 2) * DB + d + 1))
                        dve.scalar_tensor_tensor(shift[:, d, :], xbuf[:, d, j:j + N], convw_s[:, d, j:j + 1], shift[:, d, :],
                                                 ALU.mult, ALU.add).then_inc(conv_d.sem, 1)

                for j in range(1, W):
                    conv(j)
                for m in range(4):
                    layer1(m)
                dve.wait_ge(shift_hi.sem, shift_hi.at(me))
                low(partl[:], shift[:], parth[:]).then_inc(shift_lo.sem, 1)
                hid0(0)
                layer1(4)
                layer1(5)
                hid0(1)
                layer1(6)
                layer1(7)
                hid0(2)
                hid0(3)
                for c in range(NC):
                    dve.wait_ge(tanh_d.sem, tanh_d.at(me, c + 1))
                    dve.wait_ge(xt_mm.sem, xt_mm.at(me, c + 1))
                    dve.scalar_tensor_tensor(v[:, c, :], tanhv[:, c, :], 1.0, ab[c][:], ALU.add, ALU.mult).then_inc(v_d.sem, 1)
                if p == HALVES - 1:
                    dve.memset(xbuf[:, :, 0:W - 1], 0.0).then_inc(halo_d.sem, 1)
                else:
                    dve.tensor_copy(xbuf[:, :, 0:W - 1], xbuf[:, :, N:N + W - 1]).then_inc(halo_d.sem, 1)

                step = [0]

                def done(ins):
                    step[0] += 1
                    ins.then_inc(gs.sem, 1)

                def need(k):
                    dve.wait_ge(gs.sem, gs.at(me, k))

                dve.wait_ge(pr_mm.sem, pr_mm.at(me))
                dve.wait_ge(tanh_d.sem, tanh_d.at(me))
                for c in range(NC):
                    done(dve.tensor_scalar(t1[rows(c), :], ab[2][0:K, N + c * CH:N + (c + 1) * CH], projb_s[0:K, :], 0.0, ALU.add, ALU.max))
                for c in range(NC):
                    done(dve.tensor_scalar(t2[rows(c), :], ab[2][0:K, N + c * CH:N + (c + 1) * CH], projb_s[0:K, :], 0.0, ALU.add, ALU.min))
                need(2 * NC)
                done(dve.tensor_tensor(t4, t2, t1, ALU.subtract))
                assert step[0] == G_ABS
                dve.wait_ge(exp_d.sem, exp_d.at(me, 1))
                done(dve.tensor_scalar(bsum, t4, poly[LOG_DEG], None, ALU.mult))
                for i in range(LOG_DEG - 1, 0, -1):
                    need(step[0])
                    done(dve.scalar_tensor_tensor(bsum, bsum, poly[i], t4, ALU.add, ALU.mult))
                assert step[0] == G_POLY
                need(step[0])
                dve.wait_ge(exp_d.sem, exp_d.at(me, 2))
                done(dve.scalar_tensor_tensor(t5, bsum, poly[0], t5, ALU.add, ALU.mult))
                done(dve.scalar_tensor_tensor(t4, bsum, poly[0], t4, ALU.add, ALU.mult))
                need(step[0])
                done(dve.tensor_tensor(bsum, t4, t1, ALU.add))
                done(dve.tensor_tensor(t5, t5, t1, ALU.add))
                dve.wait_ge(qk_ev.sem, qk_ev.at(me, NC))
                done(dve.tensor_scalar(t3, t3, 1.0, 0.5, ALU.add, ALU.mult))
                need(step[0])
                done(dve.tensor_tensor(t1, bsum, t3, ALU.mult))
                dve.wait_ge(ln_d.sem, ln_d.at(me))
                done(dve.tensor_tensor(t2, t5, t2, ALU.add))
                need(step[0])
                done(dve.tensor_tensor(t2, t2, t3, ALU.mult))
                done(dve.tensor_tensor_scan(bsum, ones[:], t1, 0.0, ALU.mult, ALU.add))
                need(step[0])
                done(dve.tensor_scalar(nbt[:], bsum[:, CH - 1:CH], -1.0, None, ALU.mult))
                for i in range(LEVELS):
                    m = CH >> (i + 1)
                    bl, ll = levels(bsum, m), levels(lev[:, i, :], m)
                    mid = bl[:, :, 0, m - 1:m].to_broadcast([P, CH // (2 * m), m])
                    dve.tensor_tensor(ll[:, :, 0, :], mid, bl[:, :, 0, :], ALU.subtract)
                    arg = dve.tensor_tensor(ll[:, :, 1, :], bl[:, :, 1, :], mid, ALU.subtract)
                arg.then_inc(levarg_d.sem, 1)
                dve.wait_ge(it_d.sem, it_d.at(me))
                dve.wait_ge(qk_ev.sem, qk_ev.at(me, 3 * NC))
                done(dve.tensor_tensor(k_s, k_s, t2, ALU.mult))
                need(step[0])
                assert step[0] == gs.n
                dve.wait_ge(dec_d.sem, dec_d.at(me))
                dve.tensor_tensor(t5, k_s, t5, ALU.mult).then_inc(kd_d.sem, 1)
                dve.tensor_tensor(t1, q_s, t1, ALU.mult).then_inc(qd_d.sem, 1)
                dve.wait_ge(lev_d.sem, lev_d.at(me))
                for i in range(LEVELS):
                    m = CH >> (i + 1)
                    lq = dve.tensor_tensor(levq[:, i, :].rearrange("p (b r) -> p b r", r=m), levels(lev[:, i, :], m)[:, :, 1, :],
                                           levels(q_s, m)[:, :, 1, :], ALU.mult)
                lq.then_inc(levq_d.sem, 1)
                dve.wait_ge(levq_d.sem, levq_d.at(me))
                dve.tensor_tensor(lev[:], lev[:], k_s.unsqueeze(1).to_broadcast([P, LEVELS, CH]), ALU.mult).then_inc(levk_d.sem, 1)
                dve.wait_ge(dg_mm.sem, dg_mm.at(me))
                dve.tensor_scalar(ssk[:], ab[3][:, N:N + NC], KEPS2, None, ALU.max).then_inc(ss_d.sem, 1)
                dve.wait_ge(rkn_d.sem, rkn_d.at(me))
                for c in range(NC):
                    dve.scalar_tensor_tensor(att[:, c, :], own(c), rkn[:, c:c + 1], ident_s[:],
                                             ALU.mult, ALU.mult).then_inc(att_d.sem, 1)
                for c in range(NC):
                    dve.wait_ge(lv_mm.sem, lv_mm.at(me, c + 1))
                    dve.scalar_tensor_tensor(mprod[:, c, :, :].rearrange("p l u -> p (l u)"), ab[c][:, 0:LEVELS * UP], rkn[:, c:c + 1],
                                             masks_s[:].rearrange("p l u -> p (l u)"), ALU.mult, ALU.mult).then_inc(mask_d.sem, 1)
                dve.wait_ge(mask_d.sem, mask_d.at(me))
                for i in range(LEVELS):
                    m = CH >> (i + 1)
                    dve.wait_ge(att_d.sem, att_d.at(me, NC + i))
                    upper = att[:].rearrange("p c (b u r) -> p c b u r", u=2, r=m)[:, :, :, 1, :]
                    dve.tensor_tensor(upper, upper, mprod[:, :, i, :].rearrange("p c (b r) -> p c b r", r=m), ALU.add).then_inc(att_d.sem, 1)

                def hidden_low(dst, hi, b, done_hi, done_lo):
                    dve.wait_ge(done_hi.sem, done_hi.at(me, b + 1))
                    low(dst[:, 2 * b:2 * b + 2, :], raw[:, b % 2, :, :], hi[:, 2 * b:2 * b + 2, :]).then_inc(done_lo.sem, 1)

                for b in range(4):
                    hidden_low(hid1l, hid1h, b, hid1_hi, hid1_lo)
                if not (last and p == HALVES - 1):
                    statistics(me)
                    dve.wait_ge(stat_d.sem, stat_d.at(me, 2))

                def outputs(c):
                    t = slice(c * CH, (c + 1) * CH)
                    dve.wait_ge(ot_mm.sem, ot_mm.at(me, c + 1))
                    for d in range(DB):
                        o = dve.scalar_tensor_tensor(shift[:, d, t], shift[:, d, t], resw_s[:, d:d + 1], ab[c][:, d * CH:(d + 1) * CH],
                                                     ALU.mult, ALU.add)
                    o.then_inc(o_d.sem, 1)

                def update(c):
                    dve.wait_ge(su_mm.sem, su_mm.at(me, c + 1))
                    new = ab[3 - c][rows(c), :]
                    if p == 0 and c == 0:
                        dve.tensor_copy(state[rows(1), :], new).then_inc(st_d.sem, 1)
                    else:
                        dve.wait_ge(st_d.sem, st_d.at(me, 1) if c else st_d.at(prev, 2))
                        dve.scalar_tensor_tensor(state[rows(1 - c), :], state[rows(c), :], decay[rows(c), :], new, ALU.mult,
                                                 ALU.add).then_inc(st_d.sem, 1)

                outputs(0)
                update(0)
                if not (last and p == HALVES - 1):
                    variances(me)
                hidden_low(hid0l, hid0h, 0, hid2_hi, hid2_lo)
                if not (last and p == HALVES - 1):
                    normalise(me)
                hidden_low(hid0l, hid0h, 1, hid2_hi, hid2_lo)
                outputs(1)
                dve.wait_ge(o_d.sem, o_d.at(me))
                dve.tensor_tensor(sgate[:], sgate[:], shift[:], ALU.mult).then_inc(xg_d.sem, 1)
                update(1)
                hidden_low(hid0l, hid0h, 2, hid2_hi, hid2_lo)
                hidden_low(hid0l, hid0h, 3, hid2_hi, hid2_lo)
                if not (last and p == HALVES - 1):
                    ln_low(me)
                dve.wait_ge(xg_hi.sem, xg_hi.at(me))
                low(partl[:], sgate[:], parth[:]).then_inc(xg_lo.sem, 1)
                dve.wait_ge(sq_d.sem, sq_d.at(me))
                dve.tensor_reduce(sqsum, sq.rearrange("p d t -> p t d"), mybir.AxisListType.X, ALU.add).then_inc(sqsum_d.sem, 1)
                dve.wait_ge(w3_mm.sem, w3_mm.at(me))
                for c in range(NC):
                    dve.tensor_tensor(ffn[:, c, :], fb[2 * c][:, 0:H], s3_s[:], ALU.mult).then_inc(fin_d.sem, 1)
                dve.wait_ge(fin_d.sem, fin_d.at(me, 2))
                dve.tensor_tensor(xin[:, p, :, :], xin[:, p, :, :], ffn[:], ALU.add).then_inc(fin_d.sem, 1)
                dve.wait_ge(rs_mm.sem, rs_mm.at(me))
                dve.tensor_scalar(msq[:], fb[1][:, 0:NC], 1.0 / DI, EPS, ALU.mult, ALU.add).then_inc(msq_d.sem, 1)
                dve.wait_ge(fin_d.sem, fin_d.at(me, 3))
                dve.wait_ge(rms_d.sem, rms_d.at(me))
                for c in range(NC):
                    dve.scalar_tensor_tensor(xin[:, p, c, :], ab[3][:, c * H:(c + 1) * H], rms[:, c:c + 1], xin[:, p, c, :],
                                             ALU.mult, ALU.add).then_inc(fin_d.sem, 1)

            dve.wait_ge(prep_act, len(CHUNKS))
            with dve.Fori(0, B - 1) as seq:
                for p in range(HALVES):
                    half(seq, p, False)
            for p in range(HALVES):
                half(B - 1, p, True)


def kernel(**inputs):
    import numpy as _np
    import concourse.bacc as _bacc
    from concourse import mybir as _mybir
    from concourse.bass_utils import run_bass_kernel_spmd as _run

    a = {n.removeprefix("L0_"): _np.asarray(v) for n, v in inputs.items()}

    def blocks(w):
        t = w.T.reshape(-1, P, w.shape[0])
        return t.transpose(1, 0, 2).reshape(P, -1)

    def columns(s):
        return s.reshape(-1, P).T

    up, w3 = a["attn_up_w"], blocks(a["ffn_w3_w"])
    chunk = {"comb": up.reshape(DB, P, H).transpose(1, 0, 2).reshape(P, -1), "up": blocks(up), "gate": blocks(a["attn_gate_w"]),
             "proj": _np.concatenate([blocks(_np.concatenate([a["attn_q_w"], a["attn_k_w"]])),
                                      blocks(_np.concatenate([a["attn_g_w"], a["attn_tau_w"]]))], axis=1),
             "down": blocks(a["attn_down_w"]), "w30": w3[:, :STAGE], "w31": w3[:, STAGE:]}
    for name in ("w1", "w2", "h1", "h2"):
        t = blocks(a[f"ffn_{name}_w"])
        for k in range(t.shape[1] // STAGE):
            chunk[f"{name}{k}"] = t[:, k * STAGE:(k + 1) * STAGE]
    token = _np.arange(CH)
    masks = _np.zeros((P, LEVELS, UP), _np.float32)
    for i in range(LEVELS):
        m = CH >> (i + 1)
        upper = token[token // m % 2 == 1]
        masks[:, i, :] = (token[:, None] // m % 2 == 0) & (token[:, None] // (2 * m) == upper[None, :] // (2 * m))
    arrays = {
        "x": a["attn_hidden_states"].reshape(B, HALVES, NC, P, H),
        "stage_w": _np.stack([chunk[n] for n in CHUNKS]),
        "ig1t": a["attn_ig_w1"].T.reshape(DB, P, R).transpose(1, 0, 2),
        "ig2t": _np.concatenate([a["attn_ig_w2"].T, a["attn_ig_b2"][None]]),
        "convw": a["attn_conv_w"].reshape(DB, P, W).transpose(1, 0, 2),
        "convb": columns(a["attn_conv_b"]),
        "projb": _np.concatenate([a["attn_g_b"], a["attn_tau_b"]])[:, None],
        "resw": columns(a["attn_residual_weight"]),
        "normw": columns(a["attn_norm_weight"]),
        "s1": columns(a["ffn_w1_s"]), "s2": columns(a["ffn_w2_s"]),
        "sh1": columns(a["ffn_h1_s"]), "sh2": columns(a["ffn_h2_s"]),
        "s3": _np.broadcast_to(a["ffn_w3_s"], (P, H)),
        "ident": _np.eye(P, dtype=_np.float32),
        "masks": masks,
    }
    nc = _bacc.Bacc("TRN2", target_bir_lowering=False, num_devices=1, dynamic_dma_scratch_size=1024)
    args = []
    for name, v in arrays.items():
        arrays[name] = v = _np.ascontiguousarray(v)
        args.append(nc.dram_tensor(name, v.shape, _mybir.dt.from_np(v.dtype), kind="ExternalInput").ap())
    args[0] = args[0].rearrange("b h c p d -> (b h) p c d")
    out = nc.dram_tensor("out", (B, HALVES, NC, P, H), F32, kind="ExternalOutput").ap()
    layer_program(nc, *args, out.rearrange("b h c p d -> (b h) p c d"))
    r = _run(nc, [arrays], core_ids=[0])
    return r.results[0]["out"].reshape(B, T, H)
```

```python
from contextlib import ExitStack

import concourse.bass as bass
import numpy as np
from concourse import mybir

F32 = mybir.dt.float32
F32R = mybir.dt.float32r
ALU = mybir.AluOpType
ACT = mybir.ActivationFunctionType

P = 128
B, T, H = 16, 512, 256
DI, K, R, W = 512, 64, 16, 4
F = 1024
CH = 128
NC = 2
N = CH * NC
HALVES = T // N
HB, DB, FB = H // P, DI // P, F // P
LEVELS = 7
UP = CH // 2
EPS = 1e-5
KEPS2 = 1e-24
STAGE = 1024
SLOTS = 8
LOG_DEG = 10

CHUNKS = (["up"] + [f"w1{k}" for k in range(2)] + [f"w2{k}" for k in range(2)] + ["gate", "proj", "comb"]
          + [f"h1{k}" for k in range(8)] + ["down"] + [f"h2{k}" for k in range(8)] + ["w30", "w31"])
Z = 32
ZK = 2 * Z + R + 1
COMB = CHUNKS.index("comb")
SPLIT = {"up": 0, "gate": 1, "proj": 2, "down": 3}
LOADS = [(n, m) for n in ("w1", "h1", "h2") for m in range(FB)] + [("w3", 0), ("w3", 1)]
WHOLE = {n: i for i, n in enumerate(c for c in CHUNKS if c not in SPLIT and c != "comb")}


def log1p_ratio():
    e = (np.cos(np.pi * (np.arange(400) + 0.5) / 400) + 1) / 2
    c = np.polynomial.Chebyshev.fit(e, np.log1p(e) / e, LOG_DEG, domain=[0, 1])
    return [float(x) for x in c.convert(kind=np.polynomial.Polynomial).coef]


class Signal:

    def __init__(self, sem, per_half, primed=0):
        self.sem, self.n, self.primed = sem, per_half, primed

    def at(self, half, k=None):
        seq, place = half
        k = self.n if k is None else k
        return seq * (HALVES * self.n) + (place * self.n + k + self.primed)


def layer_program(nc, x, stage_w, ig1t, ig2t, convw, convb, projb, resw, normw, s1, s2, sh1, sh2, s3, ident,
                  masks, out):
    ctx = ExitStack()
    with ctx:
        def sb(name, shape, dt=F32):
            return ctx.enter_context(nc.sbuf_tensor(name, shape, dt))

        def sig(name, per_half, primed=0):
            return Signal(ctx.enter_context(nc.semaphore(name)), per_half, primed)

        def sem(name):
            return ctx.enter_context(nc.semaphore(name))

        wwhole = sb("wwhole", [P, len(WHOLE), STAGE], F32R)
        whi = sb("whi", [P, len(SPLIT), STAGE], F32R)
        wlo = sb("wlo", [P, len(SPLIT), STAGE], F32R)
        combh = sb("combh", [P, HB, R], F32R)
        combl = sb("combl", [P, HB, R], F32R)
        ig1w = sb("ig1w", [P, DB, R])
        ig2s = sb("ig2s", [ZK, DI], F32R)
        convw_s = sb("convw_s", [P, DB, W])
        convb_s = sb("convb_s", [P, DB])
        projb_s = sb("projb_s", [P, 1])
        projb_half = sb("projb_half", [P, 1])
        resw_s = sb("resw_s", [P, DB])
        normw_s = sb("normw_s", [P, DB])
        s1_s, s2_s = sb("s1_s", [P, FB]), sb("s2_s", [P, FB])
        sh1_s, sh2_s = sb("sh1_s", [P, FB]), sb("sh2_s", [P, FB])
        s3_s = sb("s3_s", [P, H])
        ident_s = sb("ident_s", [P, P])
        masks_s = sb("masks_s", [P, LEVELS, UP])
        ones = sb("ones", [P, CH])
        pair_ones = sb("pair_ones", [P, NC])
        minus_half = sb("minus_half", [P, NC])

        stream = sb("stream", [P, 2, STAGE])
        inexact = sb("inexact", [P, len(WHOLE)])
        inexact_sum = sb("inexact_sum", [P, 1])
        general = sb("general", [1, 1], mybir.dt.int32)

        xin = sb("xin", [P, HALVES, NC, H])
        xnth, xntl = sb("xnth", [P, HB, N], F32R), sb("xntl", [P, HB, N], F32R)
        hid0h, hid0l = sb("hid0h", [P, FB, N], F32R), sb("hid0l", [P, FB, N], F32R)
        hid1h, hid1l = sb("hid1h", [P, FB, N], F32R), sb("hid1l", [P, FB, N], F32R)
        mixed = sb("mixed", [P, 4 * N])
        silu1 = mixed[:].rearrange("p (a t) -> p a t", a=4)
        mprod = mixed[:, 0:NC * LEVELS * UP].rearrange("p (c l u) -> p c l u", c=NC, l=LEVELS)
        ffn = mixed[:, 0:NC * H].rearrange("p (c h) -> p c h", c=NC)
        raw = sb("raw", [P, 2, 2, N])
        xbuf = sb("xbuf", [P, DB, W - 1 + N])
        shift = sb("shift", [P, DB, N])
        parth, partl = sb("parth", [P, DB, N], F32R), sb("partl", [P, DB, N], F32R)
        sgate = sb("sgate", [P, DB, N])
        zs = sb("zs", [ZK, N], F32R)
        v = sb("v", [P, NC, DI])
        small = sb("small", [P, 8, CH])
        work = sb("work", [P, DB * N + NC * H + N])
        tanhv = work[:, 0:NC * DI].rearrange("p (c d) -> p c d", c=NC)
        lev = work[:, 0:LEVELS * CH].rearrange("p (l t) -> p l t", l=LEVELS)
        levq = work[:, LEVELS * CH:LEVELS * (CH + UP)].rearrange("p (l t) -> p l t", l=LEVELS)
        sq = work[:, 0:DB * N].rearrange("p (d t) -> p d t", d=DB)
        xn = work[:, DB * N:DB * N + NC * H].rearrange("p (c h) -> p c h", c=NC)
        sqsum = work[:, DB * N + NC * H:]
        att = sb("att", [P, NC, CH])
        state = sb("state", [P, DI])
        kdt = sb("kdt", [P, NC, K])
        stats = sb("stats", [P, NC, 6])
        mv = sb("mv", [P, NC, 2])
        varp, rstd = sb("varp", [P, NC]), sb("rstd", [P, NC])
        ssk, rkn = sb("ssk", [P, NC]), sb("rkn", [P, NC])
        msq, rms = sb("msq", [P, NC]), sb("rms", [P, NC])
        ig2raw = state[0:R + 1, :]
        nbt, decay = sb("nbt", [P, 1]), sb("decay", [P, 1])

        fb = [ctx.enter_context(nc.psum_tensor(f"fb{i}", [P, 512], F32)) for i in range(4)]
        ab = [ctx.enter_context(nc.psum_tensor(f"ab{i}", [P, 512], F32)) for i in range(4)]

        const_in = sem("const_in")
        stage_in = [sem(f"stage_in{i}") for i in range(SLOTS)]
        prep_act, prep_dve, prep_pe, prep_pool = sem("prep_act"), sem("prep_dve"), sem("prep_pe"), sem("prep_pool")
        flag_pe, flag_dve, ig2_d = sem("flag_pe"), sem("flag_dve"), sem("ig2_d")
        stream_in = [sem(f"stream_in{i}") for i in range(2)]
        x_in = [sem(f"x_in{i}") for i in range(HALVES)]
        x_out = [sem(f"x_out{i}") for i in range(HALVES)]
        up_mm, z_mm, l1_mm, gate_mm = sig("up_mm", 2), sig("z_mm", 1), sig("l1_mm", FB), sig("gate_mm", 2)
        xt_mm, ig_mm, pr_mm, dg_mm = sig("xt_mm", NC), sig("ig_mm", NC), sig("pr_mm", 1), sig("dg_mm", 1)
        lv_mm, kt_mm, ot_mm, su_mm = sig("lv_mm", NC), sig("kt_mm", 1), sig("ot_mm", NC), sig("su_mm", NC)
        h1_mm, h2_mm, dn_mm = sig("h1_mm", FB), sig("h2_mm", FB), sig("dn_mm", 1)
        rs_mm, ln_mm, w3_mm = sig("rs_mm", 1), sig("ln_mm", 1, 1), sig("w3_mm", 1, 1)
        x_ev, z_ev, tap0, silu_d = sig("x_ev", 2), sig("z_ev", 2), sig("tap0", DB), sig("silu_d", FB)
        hid0_hi, gate_ev, shift_d, shift_hi = sig("hid0_hi", 4), sig("gate_ev", 2), sig("shift_d", 1), sig("shift_hi", 1)
        tanh_d, qk_ev, exp_d, ln_d, it_d = sig("tanh_d", NC), sig("qk_ev", 4 * NC), sig("exp_d", 2), sig("ln_d", 1), sig("it_d", 1)
        lev_d, dec_d, kd_ev = sig("lev_d", 1), sig("dec_d", 3), sig("kd_ev", NC)
        gelu1_d, hid1_hi, gelu2_d, hid2_hi = sig("gelu1_d", FB), sig("hid1_hi", 4), sig("gelu2_d", FB), sig("hid2_hi", 4)
        sq_d, xg_hi, ln_hi = sig("sq_d", 1), sig("xg_hi", 1), sig("ln_hi", 1, 1)
        conv_d, l1_d, hid0_lo, shift_lo = sig("conv_d", DB * (W - 1)), sig("l1_d", FB), sig("hid0_lo", 4), sig("shift_lo", 1)
        z_lo = sig("z_lo", 1)
        halo_d = sig("halo_d", 1, 1)
        v_d, gs = sig("v_d", NC), sig("gs", LOG_DEG + 16 + 2 * (NC - 1))
        levarg_d, levq_d, levk_d, kd_d, qd_d = sig("levarg_d", 1), sig("levq_d", 1), sig("levk_d", 1), sig("kd_d", 1), sig("qd_d", 1)
        ss_d, att_d, mask_d = sig("ss_d", 1), sig("att_d", LEVELS + 2), sig("mask_d", NC)
        st_d, o_d, xg_d, xg_lo = sig("st_d", NC), sig("o_d", NC, NC), sig("xg_d", 1), sig("xg_lo", 1)
        sqsum_d = sig("sqsum_d", 1)
        hid1_lo, hid2_lo = sig("hid1_lo", 4), sig("hid2_lo", 4)
        msq_d, fin_d, stat_d, var_d, xn_d, ln_lo = (sig("msq_d", 1, 1), sig("fin_d", 5, 5), sig("stat_d", 3, 3),
                                                    sig("var_d", 1, 1), sig("xn_d", 1, 1), sig("ln_lo", 1, 1))
        rkn_d, rms_d, rstd_d = sig("rkn_d", 1), sig("rms_d", 1), sig("rstd_d", 1, 1)

        G_ABS = 2 * NC + 1
        G_POLY = G_ABS + LOG_DEG + 2

        q_s, k_s, bsum, t1, t2, t3, t4, t5 = (small[:, i, :] for i in range(8))
        e2, odd = att[:, 0, :], att[:, 1, :]
        CONSTS = [(ig1w, ig1t), (ig2raw, ig2t), (convw_s, convw), (convb_s, convb), (projb_s, projb), (resw_s, resw),
                  (normw_s, normw), (s1_s, s1), (s2_s, s2), (sh1_s, sh1), (sh2_s, sh2), (s3_s, s3), (ident_s, ident),
                  (masks_s, masks)]

        def stage_slot(n):
            return (sgate[:].rearrange("p d t -> p (d t)"), shift[:].rearrange("p d t -> p (d t)"),
                    v[:].rearrange("p c d -> p (c d)"), raw[:].rearrange("p a b t -> p (a b t)"), stream[:, 0, :], stream[:, 1, :],
                    mixed[:], small[:].rearrange("p a t -> p (a t)"))[n % SLOTS]

        def rows(c):
            return slice(c * K, (c + 1) * K)

        def own(c):
            return ab[3 - c][:, P:P + CH]

        def levels(ap, m):
            return ap.rearrange("p (b u r) -> p b u r", u=2, r=m)

        block = ctx.enter_context(nc.Block())

        @block.sync
        def _(sp):
            sp.sem_inc(x_out[1], 16)
            for n in range(len(CHUNKS)):
                if n == SLOTS - 1:
                    sp.dma_start(xin[:, 0, :, :], x[0]).then_inc(x_in[0], 16)
                    for dst, src in CONSTS:
                        sp.dma_start(dst if dst is ig2raw else dst[:], src).then_inc(const_in, 16)
                if n >= SLOTS:
                    sp.wait_ge(prep_act, n - SLOTS + 1)
                    sp.wait_ge(prep_dve, n - SLOTS + 1)
                sp.dma_start(stage_slot(n), stage_w[n]).then_inc(stage_in[n % SLOTS], 16)

            def load_weights(me, i):
                seq, p = me
                name, m = LOADS[i]
                if i < 2:
                    sp.wait_ge(w3_mm.sem, w3_mm.at((seq, p - 1)))
                else:
                    used, m_used = LOADS[i - 2]
                    mm = {"w1": l1_mm, "h1": h1_mm, "h2": h2_mm}[used]
                    sp.wait_ge(mm.sem, mm.at(me, m_used + 1))
                if name == "w3":
                    src, dst = stage_w[CHUNKS.index(f"w3{m}")], stream[:, i % 2, :]
                else:
                    first, n = CHUNKS.index(name + "0"), 4 if name == "w1" else FB
                    src = stage_w[first:first + n, :, m * P:(m + 1) * P].rearrange("k p o -> p k o")
                    dst = stream[:, i % 2, 0:n * P].rearrange("p (k o) -> p k o", k=n)
                sp.dma_start(dst, src).then_inc(stream_in[i % 2], 16)

            def half(seq, p, last, exact):
                me = (seq, p)
                if not (last and p == HALVES - 1):
                    if p == 0:
                        sp.wait_ge(x_out[1], seq * 16 + 16)
                        sp.dma_start(xin[:, 1, :, :], x[seq * HALVES + 1]).then_inc(x_in[1], 16)
                    else:
                        sp.wait_ge(x_out[0], seq * 16 + 16)
                        sp.dma_start(xin[:, 0, :, :], x[seq * HALVES + HALVES]).then_inc(x_in[0], 16)
                if not exact:
                    for i in range(len(LOADS)):
                        load_weights(me, i)
                sp.wait_ge(fin_d.sem, fin_d.at(me))
                sp.dma_start(out[seq * HALVES + p], xin[:, p, :, :]).then_inc(x_out[p], 16)

            def sequences(exact):
                with sp.Fori(0, B - 1) as seq:
                    for p in range(HALVES):
                        half(seq, p, False, exact)
                for p in range(HALVES):
                    half(B - 1, p, True, exact)

            sp.wait_ge(flag_dve, 2)
            inexact_weights = sp.value_load(general[0:1, 0:1])
            with sp.If(inexact_weights == 0):
                sequences(True)
            with sp.Else():
                sequences(False)
            sp.wait_ge(x_out[0], B * 16)
            sp.wait_ge(x_out[1], B * 16 + 16)

        @block.gpsimd
        def _(pool):
            pool.memset(minus_half[:], -0.5).then_inc(prep_pool, 1)
            pool.memset(ones[:], 1.0).then_inc(prep_pool, 1)
            pool.memset(xbuf[:], 0.0).then_inc(prep_pool, 1)
            pool.wait_ge(prep_pool, 1)

            def normalise(me):
                pool.wait_ge(var_d.sem, var_d.at(me))
                pool.tensor_tensor(rstd[:], varp[:], minus_half[:], ALU.pow).then_inc(rstd_d.sem, 1)

            def half(seq, p, last):
                me = (seq, p)
                pool.wait_ge(ss_d.sem, ss_d.at(me))
                pool.tensor_tensor(rkn[:], ssk[:], minus_half[:], ALU.pow).then_inc(rkn_d.sem, 1)
                if not (last and p == HALVES - 1):
                    normalise(me)
                pool.wait_ge(msq_d.sem, msq_d.at(me))
                pool.tensor_tensor(rms[:], msq[:], minus_half[:], ALU.pow).then_inc(rms_d.sem, 1)

            normalise((0, -1))
            with pool.Fori(0, B - 1) as seq:
                for p in range(HALVES):
                    half(seq, p, False)
            for p in range(HALVES):
                half(B - 1, p, True)

        @block.tensor
        def _(pe):
            def wide(o, pairs, start=True, stop=True):
                for i, (a, b) in enumerate(pairs):
                    mm = pe.matmul(o, a, b, start=start and i == 0, stop=stop and i == len(pairs) - 1)
                return mm

            def three(whi_b, wlo_b, ah, al):
                return [(whi_b, ah), (whi_b, al), (wlo_b, ah)]

            def split_w(name, k, lo, hi, width):
                i = SPLIT[name]
                return whi[:, i, k * width + lo:k * width + hi], wlo[:, i, k * width + lo:k * width + hi]

            def ffn_weight(exact, name, k, m):
                if exact:
                    return (wwhole[:, WHOLE[f"w3{k // 4}"], (k % 4) * H:(k % 4 + 1) * H] if name == "w3" else
                            wwhole[:, WHOLE[f"{name}{k}"], m * P:(m + 1) * P])
                if name == "w3":
                    return stream[:, LOADS.index((name, k // 4)) % 2, (k % 4) * H:(k % 4 + 1) * H]
                if name == "w2":
                    name, k = "w1", HB + k
                return stream[:, LOADS.index((name, m)) % 2, k * P:(k + 1) * P]

            def loaded(exact, me, name, m):
                if not exact:
                    seq, p = me
                    i = LOADS.index((name, m))
                    per_half = len(LOADS) // 2
                    pe.wait_ge(stream_in[i % 2], seq * (16 * HALVES * per_half) + 16 * (p * per_half + i // 2 + 1))

            def parts(exact, *aps):
                return aps if exact else tuple(a.bitcast(F32) for a in aps)

            pe.wait_ge(const_in, 16 * len(CONSTS))
            pe.wait_ge(stage_in[COMB % SLOTS], 16 * (COMB // SLOTS + 1))
            for h in range(HB):
                for d in range(DB):
                    mm = pe.matmul(ab[0][:, h * R:(h + 1) * R], stage_slot(COMB)[:, d * H + h * P:d * H + (h + 1) * P],
                                   ig1w[:, d, :], start=(d == 0), stop=(d == DB - 1))
            mm.then_inc(prep_pe, 1)

            def ln_transpose(me, first=False):
                pe.wait_ge(xn_d.sem, xn_d.at(me))
                if not first:
                    pe.wait_ge(st_d.sem, st_d.at(me, 2))
                for h in range(HB):
                    for c in range(NC):
                        mm = pe.transpose(ab[2][:, h * N + c * CH:h * N + (c + 1) * CH], xn[:, c, h * P:(h + 1) * P], ident_s[:])
                mm.then_inc(ln_mm.sem, 1)

            ln_transpose((0, -1), True)

            def half(seq, p, last, exact):
                me, prev = (seq, p), (seq, p - 1)
                xh, xl = xnth, xntl
                pe.wait_ge(ln_hi.sem, ln_hi.at(prev))
                pe.wait_ge(ln_lo.sem, ln_lo.at(prev))
                for b in range(2):
                    pe.wait_ge(o_d.sem, o_d.at(prev, b + 1))
                    for m in (2 * b, 2 * b + 1):
                        pairs = []
                        for k in range(HB):
                            pairs += three(*split_w("up", k, m * P, (m + 1) * P, DI), xh[:, k, :], xl[:, k, :])
                        mm = wide(ab[b][:, (m % 2) * N:(m % 2 + 1) * N], pairs)
                    mm.then_inc(up_mm.sem, 1)
                pairs = []
                for k in range(HB):
                    pairs += three(combh[:, k, :], combl[:, k, :], xh[:, k, :], xl[:, k, :])
                wide(ab[2][0:R, 0:N], pairs).then_inc(z_mm.sem, 1)

                def layer1(m):
                    if m in (0, 2):
                        pe.wait_ge(fin_d.sem, fin_d.at(prev, m // 2 + 1))
                    elif m == 1:
                        pe.wait_ge(msq_d.sem, msq_d.at(prev))
                    elif m >= 4:
                        pe.wait_ge(l1_d.sem, l1_d.at(me, m - 3))
                    loaded(exact, me, "w1", m)
                    for j, w in enumerate(("w1", "w2")):
                        pairs = []
                        for k in range(HB):
                            wb = ffn_weight(exact, w, k, m)
                            pairs += [(wb, a) for a in parts(exact, xh[:, k, :], xl[:, k, :])]
                        mm = wide(fb[m % 4][:, j * N:(j + 1) * N], pairs)
                    mm.then_inc(l1_mm.sem, 1)

                def gate(b):
                    if b == 0:
                        pe.wait_ge(z_lo.sem, z_lo.at(me))
                    else:
                        pe.wait_ge(fin_d.sem, fin_d.at(prev))
                    for m in (2 * b, 2 * b + 1):
                        pairs = []
                        for k in range(HB):
                            pairs += three(*split_w("gate", k, m * P, (m + 1) * P, DI), xh[:, k, :], xl[:, k, :])
                        mm = wide(ab[2 + b][:, (m % 2) * N:(m % 2 + 1) * N], pairs)
                    mm.then_inc(gate_mm.sem, 1)

                for m in range(4):
                    layer1(m)
                gate(0)
                gate(1)
                def input_gate(c):
                    if c == 1:
                        pe.wait_ge(gate_ev.sem, gate_ev.at(me))
                    pe.wait_ge(z_lo.sem, z_lo.at(me))
                    pe.matmul(ab[2 + c][:], zs[:, c * CH:(c + 1) * CH], ig2s[:], start=True, stop=True).then_inc(ig_mm.sem, 1)

                for m in range(4, FB):
                    if m == FB - 2:
                        pe.wait_ge(gate_ev.sem, gate_ev.at(me, 1))
                        input_gate(0)
                    layer1(m)
                for c in range(NC):
                    pe.wait_ge(x_ev.sem, x_ev.at(me))
                    for d in range(DB):
                        mm = pe.transpose(ab[c][:, d * P:(d + 1) * P], xbuf[:, d, W - 1 + c * CH:W - 1 + (c + 1) * CH], ident_s[:])
                    mm.then_inc(xt_mm.sem, 1)
                input_gate(1)
                pe.wait_ge(shift_hi.sem, shift_hi.at(me))
                pe.wait_ge(shift_lo.sem, shift_lo.at(me))
                pe.wait_ge(tanh_d.sem, tanh_d.at(me, 1))
                for j in range(2):
                    pairs = []
                    for k in range(DB):
                        lo = j * DI + k * P
                        pairs += three(whi[:, SPLIT["proj"], lo:lo + P], wlo[:, SPLIT["proj"], lo:lo + P], parth[:, k, :], partl[:, k, :])
                    mm = wide(ab[2][:, j * N:(j + 1) * N], pairs)
                mm.then_inc(pr_mm.sem, 1)

                def hidden(name, b, ih, il, done, in_hi, in_lo):
                    for m in (2 * b, 2 * b + 1):
                        loaded(exact, me, name, m)
                        for k in range(FB):
                            if name == "h2" and m == 0 and k == FB // 2:
                                level_scores(1)
                            if m == 0 and k % 2 == 0:
                                pe.wait_ge(in_hi.sem, in_hi.at(me, k // 2 + 1))
                                pe.wait_ge(in_lo.sem, in_lo.at(me, k // 2 + 1))
                            wb = ffn_weight(exact, name, k, m)
                            mm = wide(fb[b][:, (m % 2) * N:(m % 2 + 1) * N],
                                      [(wb, a) for a in parts(exact, ih[:, k, :], il[:, k, :])], start=(k == 0), stop=(k == FB - 1))
                        mm.then_inc(done.sem, 1)

                for b in range(4):
                    pe.wait_ge(l1_d.sem, l1_d.at(me, b + 5))
                    hidden("h1", b, hid0h, hid0l, h1_mm, hid0_hi, hid0_lo)
                pe.wait_ge(gs.sem, gs.at(me))
                pe.wait_ge(qk_ev.sem, qk_ev.at(me))
                pe.wait_ge(tanh_d.sem, tanh_d.at(me, 2))
                pe.wait_ge(kd_d.sem, kd_d.at(me))
                pe.transpose(ab[2][:, 0:P], t5, ident_s[:]).then_inc(kt_mm.sem, 1)
                pe.matmul(ab[3][:, N:N + NC], t4, pair_ones[:], start=True, stop=True)
                for c in range(NC):
                    mm = pe.matmul(own(c), k_s[rows(c), :], q_s[rows(c), :], start=True, stop=True)
                mm.then_inc(dg_mm.sem, 1)
                def level_scores(c):
                    pe.wait_ge(v_d.sem, v_d.at(me, c + 1))
                    pe.wait_ge(levq_d.sem, levq_d.at(me))
                    pe.wait_ge(levk_d.sem, levk_d.at(me))
                    for i in range(LEVELS):
                        mm = pe.matmul(ab[c][:, i * UP:(i + 1) * UP], lev[rows(c), i, :], levq[rows(c), i, :], start=True, stop=True)
                    mm.then_inc(lv_mm.sem, 1)

                level_scores(0)

                def outputs(c):
                    pe.wait_ge(mask_d.sem, mask_d.at(me, c + 1))
                    pe.wait_ge(att_d.sem, att_d.at(me))
                    carried = not (p == 0 and c == 0)
                    if carried:
                        pe.wait_ge(st_d.sem, st_d.at(me, 1) if c else st_d.at(prev, 2))
                        pe.wait_ge(qd_d.sem, qd_d.at(me))
                    for d in range(DB):
                        mm = pe.matmul(ab[c][:, d * CH:(d + 1) * CH], v[:, c, d * P:(d + 1) * P], att[:, c, :],
                                       start=True, stop=not carried)
                        if carried:
                            mm = pe.matmul(ab[c][:, d * CH:(d + 1) * CH], state[rows(c), d * P:(d + 1) * P], t1[rows(c), :],
                                           start=False, stop=True)
                    mm.then_inc(ot_mm.sem, 1)
                    pe.wait_ge(kd_ev.sem, kd_ev.at(me))
                    pe.matmul(ab[3 - c][rows(c), :], kdt[:, c, :], v[:, c, :], start=True, stop=True).then_inc(su_mm.sem, 1)

                for b in range(4):
                    pe.wait_ge(gelu1_d.sem, gelu1_d.at(me, 2 * b + 2))
                    hidden("h2", b, hid1h, hid1l, h2_mm, hid1_hi, hid1_lo)
                    if b in (1, 2):
                        outputs(b - 1)
                if not (last and p == HALVES - 1):
                    ln_transpose(me)
                for k in range(FB):
                    if k % 2 == 0:
                        pe.wait_ge(hid2_hi.sem, hid2_hi.at(me, k // 2 + 1))
                        pe.wait_ge(hid2_lo.sem, hid2_lo.at(me, k // 2 + 1))
                    if k == 0:
                        pe.wait_ge(gelu2_d.sem, gelu2_d.at(me, 6))
                    if k % 4 == 0:
                        loaded(exact, me, "w3", k // 4)
                    wb = ffn_weight(exact, "w3", k, None)
                    for c in range(NC):
                        t = slice(c * CH, (c + 1) * CH)
                        mm = wide(fb[2 * c][:, 0:H], [(a, wb) for a in parts(exact, hid0h[:, k, t], hid0l[:, k, t])],
                                  start=(k == 0), stop=(k == FB - 1))
                mm.then_inc(w3_mm.sem, 1)
                pe.wait_ge(xg_hi.sem, xg_hi.at(me))
                pe.wait_ge(xg_lo.sem, xg_lo.at(me))
                pe.wait_ge(st_d.sem, st_d.at(me, 1))
                for c in range(NC):
                    t = slice(c * CH, (c + 1) * CH)
                    pairs = []
                    for k in range(DB):
                        wh, wl = split_w("down", k, 0, H, H)
                        pairs += [(parth[:, k, t], wh), (partl[:, k, t], wh), (parth[:, k, t], wl)]
                    mm = wide(ab[3][:, c * H:(c + 1) * H], pairs)
                mm.then_inc(dn_mm.sem, 1)
                pe.wait_ge(sqsum_d.sem, sqsum_d.at(me))
                pe.wait_ge(gelu2_d.sem, gelu2_d.at(me, 4))
                for c in range(NC):
                    mm = pe.matmul(fb[1][:, c:c + 1], sqsum[:, c * CH:(c + 1) * CH], ones[:, 0:1], start=True, stop=True)
                mm.then_inc(rs_mm.sem, 1)

            def sequences(exact):
                with pe.Fori(0, B - 1) as seq:
                    for p in range(HALVES):
                        half(seq, p, False, exact)
                for p in range(HALVES):
                    half(B - 1, p, True, exact)

            pe.wait_ge(prep_pool, 3)
            pe.wait_ge(flag_dve, 1)
            pe.matmul(fb[0][0:1, 0:1], inexact_sum[:], ones[:, 0:1], start=True, stop=True).then_inc(flag_pe, 1)
            pe.wait_ge(flag_dve, 2)
            inexact_weights = pe.value_load(general[0:1, 0:1])
            with pe.If(inexact_weights == 0):
                sequences(True)
            with pe.Else():
                sequences(False)

        @block.scalar
        def _(act):
            def ln_high(me):
                act.wait_ge(ln_mm.sem, ln_mm.at(me))
                if me[1] >= 0:
                    act.wait_ge(l1_mm.sem, l1_mm.at(me))
                act.activation(xnth[:], ab[2][:].rearrange("p (h t) -> p h t", h=HB), ACT.Copy).then_inc(ln_hi.sem, 1)

            for n, name in enumerate(CHUNKS):
                if name == "comb":
                    act.wait_ge(const_in, 16 * len(CONSTS))
                    act.wait_ge(prep_pe, 1)
                    act.activation(combh[:], ab[0][:, 0:HB * R].rearrange("p (h r) -> p h r", h=HB), ACT.Copy).then_inc(prep_act, 1)
                    continue
                if n == COMB + 6:
                    ln_high((0, -1))
                act.wait_ge(stage_in[n % SLOTS], 16 * (n // SLOTS + 1))
                if name == "down":
                    for d in range(DB):
                        mul = act.activation(whi[:, SPLIT[name], d * H:(d + 1) * H], stage_slot(n)[:, d * H:(d + 1) * H], ACT.Copy,
                                             scale=normw_s[:, d:d + 1])
                    mul.then_inc(prep_act, 1)
                elif name in SPLIT:
                    act.activation(whi[:, SPLIT[name], :], stage_slot(n), ACT.Copy).then_inc(prep_act, 1)
                else:
                    act.activation(wwhole[:, WHOLE[name], :], stage_slot(n), ACT.Copy).then_inc(prep_act, 1)

            def half(seq, p, last):
                me, prev = (seq, p), (seq, p - 1)

                act.preload_act_table_set("silu_and_others")
                for b in range(2):
                    act.wait_ge(up_mm.sem, up_mm.at(me, b + 1))
                    if b == 0:
                        act.wait_ge(halo_d.sem, halo_d.at(prev))
                    act.activation(xbuf[:, 2 * b:2 * b + 2, W - 1:], ab[b][:].rearrange("p (d t) -> p d t", d=2), ACT.Copy).then_inc(x_ev.sem, 1)
                    act.wait_ge(x_ev.sem, x_ev.at(me, b + 1))
                    for d in (2 * b, 2 * b + 1):
                        act.activation(shift[:, d, :], xbuf[:, d, 0:N], ACT.Identity, bias=convb_s[:, d:d + 1],
                                       scale=convw_s[:, d, 0:1]).then_inc(tap0.sem, 1)
                act.wait_ge(z_mm.sem, z_mm.at(me))
                for part in (0, 2):
                    act.activation(zs[Z * part:Z * part + R, :], ab[2][0:R, 0:N], ACT.Copy).then_inc(z_ev.sem, 1)

                def high(src, dst, b, done):
                    act.activation(dst[:, 2 * b:2 * b + 2, :], src, ACT.Copy).then_inc(done.sem, 1)

                def silu(m):
                    if m == 0:
                        act.wait_ge(fin_d.sem, fin_d.at(prev, 3))
                    act.wait_ge(l1_mm.sem, l1_mm.at(me, m + 1))
                    if m >= 4:
                        act.wait_ge(l1_d.sem, l1_d.at(me, m - 3))
                    act.activation(silu1[:, m % 4, :], fb[m % 4][:, 0:N], ACT.Silu, scale=s1_s[:, m:m + 1]).then_inc(silu_d.sem, 1)

                def hid0(b):
                    act.wait_ge(l1_d.sem, l1_d.at(me, 2 * b + 2))
                    high(raw[:, b % 2, :, :], hid0h, b, hid0_hi)

                def gate(b):
                    act.wait_ge(gate_mm.sem, gate_mm.at(me, b + 1))
                    act.activation(sgate[:, 2 * b:2 * b + 2, :], ab[2 + b][:].rearrange("p (d t) -> p d t", d=2), ACT.Silu).then_inc(gate_ev.sem, 1)

                def input_gate(c):
                    act.wait_ge(ig_mm.sem, ig_mm.at(me, c + 1))
                    act.activation(tanhv[:, c, :], ab[2 + c][:], ACT.Tanh, scale=0.5).then_inc(tanh_d.sem, 1)

                for m in range(4):
                    silu(m)
                gate(0)
                hid0(0)
                act.wait_ge(conv_d.sem, conv_d.at(me))
                act.activation(shift[:], shift[:], ACT.Silu).then_inc(shift_d.sem, 1)
                silu(4)
                act.wait_ge(shift_d.sem, shift_d.at(me))
                act.activation(parth[:], shift[:], ACT.Copy).then_inc(shift_hi.sem, 1)
                gate(1)
                input_gate(0)
                hid0(1)
                silu(5)
                silu(6)
                silu(7)
                hid0(2)
                input_gate(1)
                hid0(3)
                act.wait_ge(pr_mm.sem, pr_mm.at(me))
                for c in range(NC):
                    act.activation(t3[rows(c), :], ab[2][K:P, N + c * CH:N + (c + 1) * CH], ACT.Tanh, bias=projb_half[K:P, :],
                                   scale=0.5).then_inc(qk_ev.sem, 1)
                act.preload_act_table_set("natural_log_exp_and_others")
                act.wait_ge(gs.sem, gs.at(me, G_ABS))
                act.activation(t4, t4, ACT.Exp).then_inc(exp_d.sem, 1)
                act.activation(t5, t1, ACT.Exp, scale=-1.0).then_inc(exp_d.sem, 1)
                for c in range(NC):
                    act.activation(k_s[rows(c), :], ab[2][K:P, c * CH:(c + 1) * CH], ACT.Copy).then_inc(qk_ev.sem, 1)
                for c in range(NC):
                    act.activation(q_s[rows(c), :], ab[2][0:K, c * CH:(c + 1) * CH], ACT.Copy, scale=0.5 * K ** -0.5).then_inc(qk_ev.sem, 1)
                act.wait_ge(gs.sem, gs.at(me, G_POLY + 4))
                act.activation(t5, t5, ACT.Ln).then_inc(ln_d.sem, 1)
                act.wait_ge(gs.sem, gs.at(me, G_POLY + 9))
                act.activation(t2, t2, ACT.Exp).then_inc(it_d.sem, 1)
                act.wait_ge(gs.sem, gs.at(me, G_POLY + 10))
                act.activation(t1, bsum, ACT.Exp, scale=-1.0).then_inc(dec_d.sem, 1)
                act.activation(t5, bsum, ACT.Exp, bias=nbt[:]).then_inc(dec_d.sem, 1)
                act.activation(decay[:], nbt[:], ACT.Exp).then_inc(dec_d.sem, 1)
                for c in range(NC):
                    act.activation(t4[rows(c), :], ab[2][K:P, c * CH:(c + 1) * CH], ACT.Square).then_inc(qk_ev.sem, 1)
                act.wait_ge(levarg_d.sem, levarg_d.at(me))
                act.activation(lev[:], lev[:], ACT.Exp, scale=-1.0).then_inc(lev_d.sem, 1)
                act.preload_act_table_set("gelu_and_others")
                def gelu(mm, scales, dst, b, done, done_hi, free):
                    act.wait_ge(mm.sem, mm.at(me, 2 * b + 2))
                    if free is not None:
                        act.wait_ge(*free)
                    for j in range(2):
                        act.activation(raw[:, b % 2, j, :], fb[b][:, j * N:(j + 1) * N], ACT.Gelu,
                                       scale=scales[:, 2 * b + j:2 * b + j + 1]).then_inc(done.sem, 1)
                    act.wait_ge(done.sem, done.at(me, 2 * b + 2))
                    high(raw[:, b % 2, :, :], dst, b, done_hi)

                for b in range(4):
                    lo = (hid0_lo, b + 3) if b < 2 else (hid1_lo, b - 1)
                    gelu(h1_mm, sh1_s, hid1h, b, gelu1_d, hid1_hi, (lo[0].sem, lo[0].at(me, lo[1])))
                act.wait_ge(rkn_d.sem, rkn_d.at(me))
                act.wait_ge(att_d.sem, att_d.at(me, NC))
                for c in range(NC):
                    act.activation(kdt[:, c, :], ab[2][:, c * K:(c + 1) * K], ACT.Copy, scale=rkn[:, c:c + 1]).then_inc(kd_ev.sem, 1)
                for b in range(4):
                    lo = (hid1_lo, b + 3) if b < 2 else (hid2_lo, b - 1)
                    if b == 3:
                        act.wait_ge(xg_d.sem, xg_d.at(me))
                        act.activation(parth[:], sgate[:], ACT.Copy).then_inc(xg_hi.sem, 1)
                    gelu(h2_mm, sh2_s, hid0h, b, gelu2_d, hid2_hi, (lo[0].sem, lo[0].at(me, lo[1])))
                if not (last and p == HALVES - 1):
                    ln_high(me)
                act.activation(sq[:], sgate[:], ACT.Square).then_inc(sq_d.sem, 1)

            act.wait_ge(prep_dve, len(CHUNKS))
            with act.Fori(0, B - 1) as seq:
                for p in range(HALVES):
                    half(seq, p, False)
            for p in range(HALVES):
                half(B - 1, p, True)

        @block.vector
        def _(dve):
            poly = log1p_ratio()
            for s in (o_d, fin_d, msq_d, halo_d, w3_mm):
                dve.sem_inc(s.sem, s.primed)

            def low(dst, src, hi):
                return dve.tensor_tensor(dst, src, hi.bitcast(F32), ALU.subtract)

            def statistics(me):
                seq, p = me
                if p == -1:
                    nxt = 0
                    dve.wait_ge(x_in[0], 16)
                else:
                    nxt = 1 - p
                    dve.wait_ge(x_in[nxt], seq * 16 + (16 if p == 0 else 32))
                for c in range(NC):
                    dve.bn_stats(stats[:, c, :], xin[:, nxt, c, :]).then_inc(stat_d.sem, 1)

            def variances(me):
                for c in range(NC):
                    ag = dve.bn_aggr(mv[:, c, :], stats[:, c, :])
                ag.then_inc(stat_d.sem, 1)
                dve.wait_ge(stat_d.sem, stat_d.at(me, 3))
                dve.tensor_scalar(varp[:], mv[:, :, 1], EPS, None, ALU.add).then_inc(var_d.sem, 1)

            def normalise(me):
                seq, p = me
                nxt = 0 if p == -1 else 1 - p
                dve.wait_ge(rstd_d.sem, rstd_d.at(me))
                for c in range(NC):
                    ts = dve.tensor_scalar(xn[:, c, :], xin[:, nxt, c, :], mv[:, c, 0:1], rstd[:, c:c + 1], ALU.subtract, ALU.mult)
                ts.then_inc(xn_d.sem, 1)

            def ln_low(me):
                dve.wait_ge(ln_hi.sem, ln_hi.at(me))
                low(xntl[:], ab[2][:].rearrange("p (h t) -> p h t", h=HB), xnth[:]).then_inc(ln_lo.sem, 1)

            flags = hid0l[:].rearrange("p (a f) t -> p a (f t)", a=2)
            for n, name in enumerate(CHUNKS):
                if name == "comb":
                    dve.wait_ge(const_in, 16 * len(CONSTS))
                    dve.wait_ge(prep_pe, 1)
                    dve.wait_ge(prep_act, n + 1)
                    for c in range(NC):
                        for col in range(NC):
                            dve.memset(pair_ones[rows(c), col:col + 1], float(c == col))
                    dve.wait_ge(prep_pool, 3)
                    for part in range(3):
                        t = slice(Z * part, min(Z * (part + 1), ZK))
                        dve.tensor_scalar(zs[t, :], xbuf[t, 0, 0:N], float(part != 1), None, ALU.add)
                    dve.tensor_copy(ig2s[:].rearrange("p (a t) -> p a t", a=2), xbuf[0:ZK, 0:2, 0:N]).then_inc(ig2_d, 1)
                    dve.wait_ge(ig2_d, 1)
                    for part in range(2):
                        hi = dve.tensor_copy(ig2s[Z * part:Z * part + R + 1, :], ig2raw)
                    hi.then_inc(ig2_d, 1)
                    dve.wait_ge(ig2_d, 2)
                    low(ig2s[2 * Z:ZK, :], ig2raw, ig2s[0:R + 1, :])
                    dve.tensor_scalar(projb_half[:], projb_s[:], 0.5, None, ALU.mult)
                    low(combl[:], ab[0][:, 0:HB * R].rearrange("p (h r) -> p h r", h=HB), combh[:]).then_inc(prep_dve, 1)
                    statistics((0, -1))
                    continue
                if n == COMB + 1:
                    dve.wait_ge(stat_d.sem, stat_d.at((0, -1), 2))
                    variances((0, -1))
                elif n == COMB + 4:
                    normalise((0, -1))
                elif n == COMB + 8:
                    ln_low((0, -1))
                dve.wait_ge(stage_in[n % SLOTS], 16 * (n // SLOTS + 1))
                dve.wait_ge(prep_act, n + 1)
                if name in SPLIT:
                    if name == "down":
                        for d in range(DB):
                            t = slice(d * H, (d + 1) * H)
                            st = dve.scalar_tensor_tensor(wlo[:, SPLIT[name], t], stage_slot(n)[:, t], normw_s[:, d:d + 1],
                                                          whi[:, SPLIT[name], t].bitcast(F32), ALU.mult, ALU.subtract)
                        st.then_inc(prep_dve, 1)
                    else:
                        low(wlo[:, SPLIT[name], :], stage_slot(n), whi[:, SPLIT[name], :]).then_inc(prep_dve, 1)
                else:
                    if n > 1:
                        dve.wait_ge(prep_dve, n - 1)
                    dve.scalar_tensor_tensor(flags[:, n % 2, :], stage_slot(n), 1.0, wwhole[:, WHOLE[name], :].bitcast(F32), ALU.mult,
                                             ALU.not_equal, accum_out=inexact[:, WHOLE[name]:WHOLE[name] + 1]).then_inc(prep_dve, 1)
            dve.wait_ge(prep_dve, len(CHUNKS))
            dve.tensor_reduce(inexact_sum[:], inexact[:], mybir.AxisListType.X, ALU.add).then_inc(flag_dve, 1)
            dve.wait_ge(flag_pe, 1)
            dve.tensor_copy(general[:], fb[0][0:1, 0:1]).then_inc(flag_dve, 1)

            def half(seq, p, last):
                me, prev = (seq, p), (seq, p - 1)

                def layer1(m):
                    if m >= 4:
                        dve.wait_ge(hid0_lo.sem, hid0_lo.at(me, m // 2 - 1))
                    dve.wait_ge(silu_d.sem, silu_d.at(me, m + 1))
                    dve.scalar_tensor_tensor(raw[:, (m // 2) % 2, m % 2, :], fb[m % 4][:, N:2 * N], s2_s[:, m:m + 1],
                                             silu1[:, m % 4, :], ALU.mult, ALU.mult).then_inc(l1_d.sem, 1)

                def hid0(b):
                    dve.wait_ge(hid0_hi.sem, hid0_hi.at(me, b + 1))
                    low(hid0l[:, 2 * b:2 * b + 2, :], raw[:, b % 2, :, :], hid0h[:, 2 * b:2 * b + 2, :]).then_inc(hid0_lo.sem, 1)

                def conv(j):
                    for d in range(DB):
                        if j == 1:
                            dve.wait_ge(tap0.sem, tap0.at(me, d + 1))
                        else:
                            dve.wait_ge(conv_d.sem, conv_d.at(me, (j - 2) * DB + d + 1))
                        dve.scalar_tensor_tensor(shift[:, d, :], xbuf[:, d, j:j + N], convw_s[:, d, j:j + 1], shift[:, d, :],
                                                 ALU.mult, ALU.add).then_inc(conv_d.sem, 1)

                conv(1)
                dve.wait_ge(z_ev.sem, z_ev.at(me))
                low(zs[Z:Z + R, :], ab[2][0:R, 0:N], zs[0:R, :]).then_inc(z_lo.sem, 1)
                conv(2)
                layer1(0)
                layer1(1)
                conv(3)
                layer1(2)
                layer1(3)
                hid0(0)
                layer1(4)
                dve.wait_ge(shift_hi.sem, shift_hi.at(me))
                low(partl[:], shift[:], parth[:]).then_inc(shift_lo.sem, 1)
                layer1(5)
                hid0(1)
                layer1(6)
                layer1(7)
                hid0(2)
                hid0(3)
                step = [0]

                def done(ins):
                    step[0] += 1
                    ins.then_inc(gs.sem, 1)

                def need(k):
                    dve.wait_ge(gs.sem, gs.at(me, k))

                dve.wait_ge(pr_mm.sem, pr_mm.at(me))
                dve.wait_ge(tanh_d.sem, tanh_d.at(me))
                for c in range(NC):
                    done(dve.tensor_scalar(t1[rows(c), :], ab[2][0:K, N + c * CH:N + (c + 1) * CH], projb_s[0:K, :], 0.0, ALU.add, ALU.max))
                for c in range(NC):
                    done(dve.tensor_scalar(t2[rows(c), :], ab[2][0:K, N + c * CH:N + (c + 1) * CH], projb_s[0:K, :], 0.0, ALU.add, ALU.min))
                need(2 * NC)
                done(dve.tensor_tensor(t4, t2, t1, ALU.subtract))
                assert step[0] == G_ABS
                for c in range(NC):
                    dve.wait_ge(tanh_d.sem, tanh_d.at(me, c + 1))
                    dve.wait_ge(xt_mm.sem, xt_mm.at(me, c + 1))
                    dve.scalar_tensor_tensor(v[:, c, :], tanhv[:, c, :], 1.0, ab[c][:], ALU.add, ALU.mult).then_inc(v_d.sem, 1)
                if p == HALVES - 1:
                    dve.memset(xbuf[:, :, 0:W - 1], 0.0).then_inc(halo_d.sem, 1)
                else:
                    dve.tensor_copy(xbuf[:, :, 0:W - 1], xbuf[:, :, N:N + W - 1]).then_inc(halo_d.sem, 1)

                dve.wait_ge(exp_d.sem, exp_d.at(me, 1))
                done(dve.tensor_tensor(e2, t4, t4, ALU.mult))
                need(step[0])
                done(dve.tensor_scalar(bsum, e2, poly[LOG_DEG], None, ALU.mult))
                done(dve.tensor_scalar(odd, e2, poly[LOG_DEG - 1], None, ALU.mult))
                for i in range(LOG_DEG - 2, 1, -2):
                    need(step[0] - 1)
                    done(dve.scalar_tensor_tensor(bsum, bsum, poly[i], e2, ALU.add, ALU.mult))
                    need(step[0] - 1)
                    done(dve.scalar_tensor_tensor(odd, odd, poly[i - 1], e2 if i > 2 else t4, ALU.add, ALU.mult))
                need(step[0])
                done(dve.scalar_tensor_tensor(bsum, bsum, poly[0], odd, ALU.add, ALU.add))
                assert step[0] == G_POLY
                need(step[0])
                dve.wait_ge(exp_d.sem, exp_d.at(me, 2))
                done(dve.tensor_tensor(t5, bsum, t5, ALU.mult))
                done(dve.tensor_tensor(t4, bsum, t4, ALU.mult))
                need(step[0])
                done(dve.tensor_tensor(bsum, t4, t1, ALU.add))
                done(dve.tensor_tensor(t5, t5, t1, ALU.add))
                dve.wait_ge(qk_ev.sem, qk_ev.at(me, NC))
                done(dve.tensor_scalar(t3, t3, 1.0, 0.5, ALU.add, ALU.mult))
                need(step[0])
                done(dve.tensor_tensor(t1, bsum, t3, ALU.mult))
                dve.wait_ge(ln_d.sem, ln_d.at(me))
                done(dve.tensor_tensor(t2, t5, t2, ALU.add))
                need(G_POLY + 6)
                done(dve.tensor_tensor_scan(bsum, ones[:], t1, 0.0, ALU.mult, ALU.add))
                need(G_POLY + 7)
                done(dve.tensor_tensor(t2, t2, t3, ALU.mult))
                need(G_POLY + 8)
                done(dve.tensor_scalar(nbt[:], bsum[:, CH - 1:CH], -1.0, None, ALU.mult))
                for i in range(LEVELS):
                    m = CH >> (i + 1)
                    bl, ll = levels(bsum, m), levels(lev[:, i, :], m)
                    mid = bl[:, :, 0, m - 1:m].to_broadcast([P, CH // (2 * m), m])
                    dve.tensor_tensor(ll[:, :, 0, :], mid, bl[:, :, 0, :], ALU.subtract)
                    arg = dve.tensor_tensor(ll[:, :, 1, :], bl[:, :, 1, :], mid, ALU.subtract)
                arg.then_inc(levarg_d.sem, 1)
                dve.wait_ge(it_d.sem, it_d.at(me))
                dve.wait_ge(qk_ev.sem, qk_ev.at(me, 3 * NC))
                done(dve.tensor_tensor(k_s, k_s, t2, ALU.mult))
                need(step[0])
                assert step[0] == gs.n
                dve.wait_ge(dec_d.sem, dec_d.at(me))
                dve.tensor_tensor(t5, k_s, t5, ALU.mult).then_inc(kd_d.sem, 1)
                dve.tensor_tensor(t1, q_s, t1, ALU.mult).then_inc(qd_d.sem, 1)
                dve.wait_ge(lev_d.sem, lev_d.at(me))
                for i in range(LEVELS):
                    m = CH >> (i + 1)
                    lq = dve.tensor_tensor(levq[:, i, :].rearrange("p (b r) -> p b r", r=m), levels(lev[:, i, :], m)[:, :, 1, :],
                                           levels(q_s, m)[:, :, 1, :], ALU.mult)
                lq.then_inc(levq_d.sem, 1)
                dve.wait_ge(levq_d.sem, levq_d.at(me))
                dve.tensor_tensor(lev[:], lev[:], k_s.unsqueeze(1).to_broadcast([P, LEVELS, CH]), ALU.mult).then_inc(levk_d.sem, 1)
                def hidden_low(dst, hi, b, done_hi, done_lo):
                    dve.wait_ge(done_hi.sem, done_hi.at(me, b + 1))
                    low(dst[:, 2 * b:2 * b + 2, :], raw[:, b % 2, :, :], hi[:, 2 * b:2 * b + 2, :]).then_inc(done_lo.sem, 1)

                def masked(c):
                    dve.wait_ge(lv_mm.sem, lv_mm.at(me, c + 1))
                    dve.scalar_tensor_tensor(mprod[:, c, :, :].rearrange("p l u -> p (l u)"), ab[c][:, 0:LEVELS * UP], rkn[:, c:c + 1],
                                             masks_s[:].rearrange("p l u -> p (l u)"), ALU.mult, ALU.mult).then_inc(mask_d.sem, 1)

                hidden_low(hid1l, hid1h, 0, hid1_hi, hid1_lo)
                dve.wait_ge(dg_mm.sem, dg_mm.at(me))
                dve.tensor_scalar(ssk[:], ab[3][:, N:N + NC], KEPS2, None, ALU.max).then_inc(ss_d.sem, 1)
                hidden_low(hid1l, hid1h, 1, hid1_hi, hid1_lo)
                dve.wait_ge(rkn_d.sem, rkn_d.at(me))
                for c in range(NC):
                    dve.scalar_tensor_tensor(att[:, c, :], own(c), rkn[:, c:c + 1], ident_s[:], ALU.mult, ALU.mult).then_inc(att_d.sem, 1)
                masked(0)
                hidden_low(hid1l, hid1h, 2, hid1_hi, hid1_lo)
                hidden_low(hid1l, hid1h, 3, hid1_hi, hid1_lo)
                masked(1)
                dve.wait_ge(mask_d.sem, mask_d.at(me))
                for i in range(LEVELS):
                    m = CH >> (i + 1)
                    dve.wait_ge(att_d.sem, att_d.at(me, NC + i))
                    upper = att[:].rearrange("p c (b u r) -> p c b u r", u=2, r=m)[:, :, :, 1, :]
                    dve.tensor_tensor(upper, upper, mprod[:, :, i, :].rearrange("p c (b r) -> p c b r", r=m), ALU.add).then_inc(att_d.sem, 1)
                if not (last and p == HALVES - 1):
                    statistics(me)
                    dve.wait_ge(stat_d.sem, stat_d.at(me, 2))

                def outputs(c):
                    t = slice(c * CH, (c + 1) * CH)
                    dve.wait_ge(ot_mm.sem, ot_mm.at(me, c + 1))
                    for d in range(DB):
                        o = dve.scalar_tensor_tensor(shift[:, d, t], shift[:, d, t], resw_s[:, d:d + 1], ab[c][:, d * CH:(d + 1) * CH],
                                                     ALU.mult, ALU.add)
                    o.then_inc(o_d.sem, 1)

                def update(c):
                    dve.wait_ge(su_mm.sem, su_mm.at(me, c + 1))
                    new = ab[3 - c][rows(c), :]
                    if p == 0 and c == 0:
                        dve.tensor_copy(state[rows(1), :], new).then_inc(st_d.sem, 1)
                    else:
                        dve.wait_ge(st_d.sem, st_d.at(me, 1) if c else st_d.at(prev, 2))
                        dve.scalar_tensor_tensor(state[rows(1 - c), :], state[rows(c), :], decay[rows(c), :], new, ALU.mult,
                                                 ALU.add).then_inc(st_d.sem, 1)

                outputs(0)
                update(0)
                if not (last and p == HALVES - 1):
                    variances(me)
                hidden_low(hid0l, hid0h, 0, hid2_hi, hid2_lo)
                if not (last and p == HALVES - 1):
                    normalise(me)
                hidden_low(hid0l, hid0h, 1, hid2_hi, hid2_lo)
                outputs(1)
                dve.wait_ge(o_d.sem, o_d.at(me))
                dve.tensor_tensor(sgate[:], sgate[:], shift[:], ALU.mult).then_inc(xg_d.sem, 1)
                update(1)
                hidden_low(hid0l, hid0h, 2, hid2_hi, hid2_lo)
                dve.wait_ge(xg_hi.sem, xg_hi.at(me))
                low(partl[:], sgate[:], parth[:]).then_inc(xg_lo.sem, 1)
                hidden_low(hid0l, hid0h, 3, hid2_hi, hid2_lo)
                if not (last and p == HALVES - 1):
                    ln_low(me)
                dve.wait_ge(sq_d.sem, sq_d.at(me))
                dve.tensor_reduce(sqsum, sq.rearrange("p d t -> p t d"), mybir.AxisListType.X, ALU.add).then_inc(sqsum_d.sem, 1)
                dve.wait_ge(w3_mm.sem, w3_mm.at(me))
                for c in range(NC):
                    dve.tensor_tensor(ffn[:, c, :], fb[2 * c][:, 0:H], s3_s[:], ALU.mult).then_inc(fin_d.sem, 1)
                dve.wait_ge(fin_d.sem, fin_d.at(me, 2))
                dve.tensor_tensor(xin[:, p, :, :], xin[:, p, :, :], ffn[:], ALU.add).then_inc(fin_d.sem, 1)
                dve.wait_ge(rs_mm.sem, rs_mm.at(me))
                dve.tensor_scalar(msq[:], fb[1][:, 0:NC], 1.0 / DI, EPS, ALU.mult, ALU.add).then_inc(msq_d.sem, 1)
                dve.wait_ge(fin_d.sem, fin_d.at(me, 3))
                dve.wait_ge(rms_d.sem, rms_d.at(me))
                for c in range(NC):
                    dve.scalar_tensor_tensor(xin[:, p, c, :], ab[3][:, c * H:(c + 1) * H], rms[:, c:c + 1], xin[:, p, c, :],
                                             ALU.mult, ALU.add).then_inc(fin_d.sem, 1)

            with dve.Fori(0, B - 1) as seq:
                for p in range(HALVES):
                    half(seq, p, False)
            for p in range(HALVES):
                half(B - 1, p, True)


def kernel(**inputs):
    import numpy as _np
    import concourse.bacc as _bacc
    from concourse import mybir as _mybir
    from concourse.bass_utils import run_bass_kernel_spmd as _run

    a = {n.removeprefix("L0_"): _np.asarray(v) for n, v in inputs.items()}

    def blocks(w):
        t = w.T.reshape(-1, P, w.shape[0])
        return t.transpose(1, 0, 2).reshape(P, -1)

    def columns(s):
        return s.reshape(-1, P).T

    up, w3 = a["attn_up_w"], blocks(a["ffn_w3_w"])
    chunk = {"comb": up.reshape(DB, P, H).transpose(1, 0, 2).reshape(P, -1), "up": blocks(up), "gate": blocks(a["attn_gate_w"]),
             "proj": _np.concatenate([blocks(_np.concatenate([a["attn_q_w"], a["attn_k_w"]])),
                                      blocks(_np.concatenate([a["attn_g_w"], a["attn_tau_w"]]))], axis=1),
             "down": blocks(a["attn_down_w"]), "w30": w3[:, :STAGE], "w31": w3[:, STAGE:]}
    for name in ("w1", "w2", "h1", "h2"):
        t = blocks(a[f"ffn_{name}_w"])
        for k in range(t.shape[1] // STAGE):
            chunk[f"{name}{k}"] = t[:, k * STAGE:(k + 1) * STAGE]
    token = _np.arange(CH)
    masks = _np.zeros((P, LEVELS, UP), _np.float32)
    for i in range(LEVELS):
        m = CH >> (i + 1)
        upper = token[token // m % 2 == 1]
        masks[:, i, :] = (token[:, None] // m % 2 == 0) & (token[:, None] // (2 * m) == upper[None, :] // (2 * m))
    arrays = {
        "x": a["attn_hidden_states"].reshape(B, HALVES, NC, P, H),
        "stage_w": _np.stack([chunk[n] for n in CHUNKS]),
        "ig1t": a["attn_ig_w1"].T.reshape(DB, P, R).transpose(1, 0, 2),
        "ig2t": _np.concatenate([a["attn_ig_w2"].T, a["attn_ig_b2"][None]]),
        "convw": a["attn_conv_w"].reshape(DB, P, W).transpose(1, 0, 2),
        "convb": columns(a["attn_conv_b"]),
        "projb": _np.concatenate([a["attn_g_b"], a["attn_tau_b"]])[:, None],
        "resw": columns(a["attn_residual_weight"]),
        "normw": columns(a["attn_norm_weight"]),
        "s1": columns(a["ffn_w1_s"]), "s2": columns(a["ffn_w2_s"]),
        "sh1": columns(a["ffn_h1_s"]), "sh2": columns(a["ffn_h2_s"]),
        "s3": _np.broadcast_to(a["ffn_w3_s"], (P, H)),
        "ident": _np.eye(P, dtype=_np.float32),
        "masks": masks,
    }
    nc = _bacc.Bacc("TRN2", target_bir_lowering=False, num_devices=1, dynamic_dma_scratch_size=1024)
    args = []
    for name, v in arrays.items():
        arrays[name] = v = _np.ascontiguousarray(v)
        args.append(nc.dram_tensor(name, v.shape, _mybir.dt.from_np(v.dtype), kind="ExternalInput").ap())
    args[0] = args[0].rearrange("b h c p d -> (b h) p c d")
    out = nc.dram_tensor("out", (B, HALVES, NC, P, H), F32, kind="ExternalOutput").ap()
    layer_program(nc, *args, out.rearrange("b h c p d -> (b h) p c d"))
    r = _run(nc, [arrays], core_ids=[0])
    return r.results[0]["out"].reshape(B, T, H)
```
